# Optimizing a Trainium2 kernel written in Bass

```python
import numpy as np
import jax
import jax.numpy as jnp

def _softmax(x, axis=-1):
    return jax.nn.softmax(x, axis=axis)

def _gelu(x):
    return jax.nn.gelu(x, approximate=True)

def _silu(x):
    return jax.nn.silu(x)

def _sigmoid(x):
    return jax.nn.sigmoid(x)

def _layernorm(x, axis=-1, eps=1e-05):
    m = jnp.mean(x, axis=axis, keepdims=True)
    v = jnp.var(x, axis=axis, keepdims=True)
    return (x - m) / jnp.sqrt(v + eps)

def _scatter_add(tgt, idx, src, axis=0):
    return tgt.at[idx].add(src)

def _segment_sum(src, seg, n):
    return jax.ops.segment_sum(src, seg, n)
kernel_name = 'mk_decoder_postln_d1_seqx_r8_2929b8'

def setup_inputs(seed: int=0):
    np.random.seed(seed)
    _w = jnp.asarray

    def _rec_inputs():
        import jax
        import jax.numpy as jnp
        _rk = jax.random.key(seed)
        x = -0.0002928 + 1 * jax.random.normal(jax.random.fold_in(_rk, 1), (2, 256, 128), jnp.float32)
        _lenS = 256 - jax.random.randint(jax.random.fold_in(_rk, 7), (2,), 0, max(1, 256 // 4) + 1, jnp.int32)
        _lenS2 = 512 - jax.random.randint(jax.random.fold_in(_rk, 8), (2,), 0, max(1, 512 // 4) + 1, jnp.int32)
        _ctx_512P = jax.random.normal(jax.random.fold_in(_rk, 11), (2, 16, 64), jnp.float32)
        _ctx_512c = jax.random.dirichlet(jax.random.fold_in(_rk, 511), 0.3 * jnp.ones((16,), jnp.float32), (2, 512))
        _ctx_512t = jnp.einsum('bsk,bkd->bsd', _ctx_512c, _ctx_512P)
        _ctx_512t = _ctx_512t * jax.lax.rsqrt(jnp.mean(jnp.square(_ctx_512t)) + 1e-12) * 0.953939
        ctx_512 = 0.00222621 + 0.99962 * (_ctx_512t + 0.3 * jax.random.normal(jax.random.fold_in(_rk, 611), (2, 512, 64), jnp.float32))
        return (x, ctx_512)
    x, ctx_512 = _rec_inputs()

    def _L0_attn_setup():
        import jax, jax.numpy as jnp
        import numpy as np
        EMBED_DIM = 128
        NUM_HEADS = 16
        HEAD_DIM = EMBED_DIM // NUM_HEADS
        SCALING = HEAD_DIM ** (-0.5)
        B, T = (2, 256)
        key = jax.random.key(seed)
        ks = jax.random.split(key, 8)
        s = 0.02
        return {'hidden_states': jax.random.normal(ks[0], (B, T, EMBED_DIM), jnp.float32), 'Wq': jax.random.normal(ks[1], (EMBED_DIM, EMBED_DIM), jnp.float32) * s, 'bq': jax.random.normal(ks[2], (EMBED_DIM,), jnp.float32) * s, 'Wk': jax.random.normal(ks[3], (HEAD_DIM, EMBED_DIM), jnp.float32) * s, 'Wv': jax.random.normal(ks[4], (HEAD_DIM, EMBED_DIM), jnp.float32) * s, 'bv': jax.random.normal(ks[5], (HEAD_DIM,), jnp.float32) * s, 'Wo': jax.random.normal(ks[6], (EMBED_DIM, EMBED_DIM), jnp.float32) * s, 'bo': jax.random.normal(ks[7], (EMBED_DIM,), jnp.float32) * s}
    _L0_attn_all = _L0_attn_setup()
    _L0_attn_in = {k: v for k, v in _L0_attn_all.items() if k in ('Wq', 'bq', 'Wk', 'Wv', 'bv', 'Wo', 'bo')}
    del _L0_attn_all

    def _L0_xattn_setup():
        import jax, jax.numpy as jnp
        import numpy as np
        B, T, TC, C, CC, H = (2, 256, 64, 128, 64, 16)
        D = C // H

        def _heads(t):
            b, l, _ = t.shape
            return t.reshape(b, l, H, D).transpose(0, 2, 1, 3)
        key = jax.random.key(seed)
        ks = jax.random.split(key, 18)
        w = lambda k, i, o: jax.random.normal(k, (i, o), jnp.float32) / np.sqrt(i).astype(np.float32)
        return {'x': jax.random.normal(ks[0], (B, T, C), jnp.float32), 'cross_input': jax.random.normal(ks[1], (B, TC, CC), jnp.float32), 'Wk': w(ks[2], C, C), 'bk': jnp.zeros((C,), jnp.float32), 'Wq': w(ks[3], C, C), 'bq': jnp.zeros((C,), jnp.float32), 'Wv': w(ks[4], C, C), 'bv': jnp.zeros((C,), jnp.float32), 'Wck': w(ks[5], CC, C), 'bck': jnp.zeros((C,), jnp.float32), 'Wcq': w(ks[6], C, C), 'bcq': jnp.zeros((C,), jnp.float32), 'Wcv': w(ks[7], CC, C), 'bcv': jnp.zeros((C,), jnp.float32), 'Wp': w(ks[8], C, C), 'bp': jnp.zeros((C,), jnp.float32)}
    _L0_xattn_all = _L0_xattn_setup()
    _L0_xattn_in = {k: v for k, v in _L0_xattn_all.items() if k in ('Wk', 'bk', 'Wq', 'bq', 'Wv', 'bv', 'Wck', 'bck', 'Wcq', 'bcq', 'Wcv', 'bcv', 'Wp', 'bp')}
    del _L0_xattn_all

    def _L0_ffn_setup():
        import jax, jax.numpy as jnp
        import numpy as np
        TOP_K = 2
        EPS = 1e-09
        key = jax.random.key(seed)
        ks = jax.random.split(key, 6)
        B, T, D, H, E = (4, 256, 128, 256, 8)
        x = jax.random.normal(ks[0], (B, T, D), dtype=jnp.float32)
        Wg = jax.random.normal(ks[1], (E, D), dtype=jnp.float32) * 0.02
        W1 = jax.random.normal(ks[2], (E, 2 * H, D), dtype=jnp.float32) * 0.02
        b1 = jax.random.normal(ks[3], (E, 2 * H), dtype=jnp.float32) * 0.02
        Wo = jax.random.normal(ks[4], (D, H), dtype=jnp.float32) * 0.02
        bo = jax.random.normal(ks[5], (D,), dtype=jnp.float32) * 0.02
        return {'x': x, 'Wg': Wg, 'W1': W1, 'b1': b1, 'Wo': Wo, 'bo': bo}
    _L0_ffn_all = _L0_ffn_setup()
    _L0_ffn_in = {k: v for k, v in _L0_ffn_all.items() if k in ('Wg', 'W1', 'b1', 'Wo', 'bo')}
    del _L0_ffn_all
    return {'x': x, 'ctx_512': ctx_512, 'L0_attn_Wq': _L0_attn_in['Wq'], 'L0_attn_bq': _L0_attn_in['bq'], 'L0_attn_Wk': _L0_attn_in['Wk'], 'L0_attn_Wv': _L0_attn_in['Wv'], 'L0_attn_bv': _L0_attn_in['bv'], 'L0_attn_Wo': _L0_attn_in['Wo'], 'L0_attn_bo': _L0_attn_in['bo'], 'L0_xattn_Wk': _L0_xattn_in['Wk'], 'L0_xattn_bk': _L0_xattn_in['bk'], 'L0_xattn_Wq': _L0_xattn_in['Wq'], 'L0_xattn_bq': _L0_xattn_in['bq'], 'L0_xattn_Wv': _L0_xattn_in['Wv'], 'L0_xattn_bv': _L0_xattn_in['bv'], 'L0_xattn_Wck': _L0_xattn_in['Wck'], 'L0_xattn_bck': _L0_xattn_in['bck'], 'L0_xattn_Wcq': _L0_xattn_in['Wcq'], 'L0_xattn_bcq': _L0_xattn_in['bcq'], 'L0_xattn_Wcv': _L0_xattn_in['Wcv'], 'L0_xattn_bcv': _L0_xattn_in['bcv'], 'L0_xattn_Wp': _L0_xattn_in['Wp'], 'L0_xattn_bp': _L0_xattn_in['bp'], 'L0_ffn_Wg': _L0_ffn_in['Wg'], 'L0_ffn_W1': _L0_ffn_in['W1'], 'L0_ffn_b1': _L0_ffn_in['b1'], 'L0_ffn_Wo': _L0_ffn_in['Wo'], 'L0_ffn_bo': _L0_ffn_in['bo']}

def reference(x, ctx_512, L0_attn_Wq, L0_attn_bq, L0_attn_Wk, L0_attn_Wv, L0_attn_bv, L0_attn_Wo, L0_attn_bo, L0_xattn_Wk, L0_xattn_bk, L0_xattn_Wq, L0_xattn_bq, L0_xattn_Wv, L0_xattn_bv, L0_xattn_Wck, L0_xattn_bck, L0_xattn_Wcq, L0_xattn_bcq, L0_xattn_Wcv, L0_xattn_bcv, L0_xattn_Wp, L0_xattn_bp, L0_ffn_Wg, L0_ffn_W1, L0_ffn_b1, L0_ffn_Wo, L0_ffn_bo):
    import jax
    import jax.numpy as jnp

    def _L0_attn_ref(hidden_states, Wq, bq, Wk, Wv, bv, Wo, bo):
        import jax, jax.numpy as jnp
        import numpy as np
        EMBED_DIM = 128
        NUM_HEADS = 16
        HEAD_DIM = EMBED_DIM // NUM_HEADS
        SCALING = HEAD_DIM ** (-0.5)
        B, T = (2, 256)
        bsz, tgt_len, _ = hidden_states.shape
        q = (hidden_states @ Wq.T + bq) * SCALING
        k = hidden_states @ Wk.T
        v = hidden_states @ Wv.T + bv
        q = q.reshape(bsz, tgt_len, NUM_HEADS, HEAD_DIM)
        scores = jnp.einsum('bthd,bsd->bhts', q, k)
        probs = jax.nn.softmax(scores, axis=-1)
        ctx = jnp.einsum('bhts,bsd->bthd', probs, v)
        ctx = ctx.reshape(bsz, tgt_len, EMBED_DIM)
        return ctx @ Wo.T + bo

    def _L0_xattn_ref(x, cross_input, Wk, bk, Wq, bq, Wv, bv, Wck, bck, Wcq, bcq, Wcv, bcv, Wp, bp):
        import jax, jax.numpy as jnp
        import numpy as np
        B, T, TC, C, CC, H = (2, 256, 64, 128, 64, 16)
        D = C // H

        def _heads(t):
            b, l, _ = t.shape
            return t.reshape(b, l, H, D).transpose(0, 2, 1, 3)
        scale = np.float32(1.0 / np.sqrt(D))
        q = _heads(x @ Wq + bq)
        k = _heads(x @ Wk + bk)
        v = _heads(x @ Wv + bv)
        att = jnp.einsum('bhqd,bhkd->bhqk', q, k) * scale
        causal = jnp.tril(jnp.ones((T, T), bool))
        att = jnp.where(causal[None, None], att, -jnp.inf)
        y = jnp.einsum('bhqk,bhkd->bhqd', jax.nn.softmax(att, axis=-1), v)
        qc = _heads(x @ Wcq + bcq)
        kc = _heads(cross_input @ Wck + bck)
        vc = _heads(cross_input @ Wcv + bcv)
        attc = jnp.einsum('bhqd,bhkd->bhqk', qc, kc) * scale
        y = y + jnp.einsum('bhqk,bhkd->bhqd', jax.nn.softmax(attc, axis=-1), vc)
        y = y.transpose(0, 2, 1, 3).reshape(x.shape[0], T, C)
        return y @ Wp + bp

    def _L0_ffn_ref(x, Wg, W1, b1, Wo, bo):
        import jax, jax.numpy as jnp
        import numpy as np
        TOP_K = 2
        EPS = 1e-09
        E = Wg.shape[0]
        gate_logits = jnp.einsum('btd,ed->bte', x, Wg)
        gate_scores = jax.nn.softmax(gate_logits, axis=-1)
        topk_val, topk_idx = jax.lax.top_k(gate_scores, TOP_K)
        topk_val = topk_val / (topk_val.sum(axis=-1, keepdims=True) + EPS)
        comb = (jax.nn.one_hot(topk_idx, E, dtype=x.dtype) * topk_val[..., None]).sum(axis=-2)
        out = jnp.zeros_like(x)
        for e in range(E):
            h = jnp.einsum('btd,hd->bth', x, W1[e]) + b1[e]
            a, b = jnp.split(h, 2, axis=-1)
            g = a * jax.nn.sigmoid(b)
            eo = jnp.einsum('bth,dh->btd', g, Wo) + bo
            out = out + eo * comb[..., e:e + 1]
        return out
    x = _layernorm(x + _L0_attn_ref(x, L0_attn_Wq, L0_attn_bq, L0_attn_Wk, L0_attn_Wv, L0_attn_bv, L0_attn_Wo, L0_attn_bo), axis=-1)
    x = _layernorm(x + _L0_xattn_ref(x, ctx_512, L0_xattn_Wk, L0_xattn_bk, L0_xattn_Wq, L0_xattn_bq, L0_xattn_Wv, L0_xattn_bv, L0_xattn_Wck, L0_xattn_bck, L0_xattn_Wcq, L0_xattn_bcq, L0_xattn_Wcv, L0_xattn_bcv, L0_xattn_Wp, L0_xattn_bp), axis=-1)
    x = _layernorm(x + _L0_ffn_ref(x, L0_ffn_Wg, L0_ffn_W1, L0_ffn_b1, L0_ffn_Wo, L0_ffn_bo), axis=-1)
    return x

_drawn_inputs = setup_inputs


def setup_inputs(seed=0):
    import zlib

    import numpy as np

    out = dict(_drawn_inputs(seed))
    spreads = {'L0_xattn_bk': (0.0, 2.0),
     'L0_xattn_bq': (0.0, 0.458),
     'L0_xattn_bv': (0.0, 0.1),
     'L0_xattn_bck': (0.0, 2.0),
     'L0_xattn_bcq': (0.0, 0.378),
     'L0_xattn_bcv': (0.0, 0.1),
     'L0_xattn_bp': (0.0, 0.1)}
    factors = {'L0_attn_Wq': 8.0,
     'L0_attn_bq': 8.0,
     'L0_attn_Wk': 8.0,
     'L0_attn_Wv': 8.0,
     'L0_attn_bv': 8.0,
     'L0_attn_Wo': 7.289,
     'L0_ffn_b1': 24.322,
     'L0_attn_bo': 4.06}
    for name, (base, spread) in spreads.items():
        noise = np.random.default_rng([zlib.crc32(name.encode()), seed]).standard_normal(out[name].shape)
        drawn = base * np.exp(spread * noise) if base else spread * noise
        out[name] = jnp.asarray(drawn.astype(out[name].dtype))
    for name, factor in factors.items():
        out[name] = (out[name] * factor).astype(out[name].dtype)
    return out
```

```python
from contextlib import ExitStack

import concourse.bass as bass
from concourse import mybir

F32 = mybir.dt.float32
BF16 = mybir.dt.bfloat16
U32 = mybir.dt.uint32
ALU = mybir.AluOpType
ACT = mybir.ActivationFunctionType
AX = mybir.AxisListType

P = 128
B, T, C, H, D = 2, 256, 128, 16, 8
TC, CC = 512, 64
E, HF = 8, 256
N = B * T
QT = T // P
SCALE = float(D) ** -0.5
EPS_LN = 1e-5
EPS_TOP = 1e-9
NEG = -1.0e30
KROWS = 96
MROW = 64
VD = D + 1
VW = 32
Q_TERMS = (0, 0, 1, 1, 0, 2)
K_TERMS = (0, 1, 0, 1, 2, 0)
NPT = 8
NROW = 4
LAG = 2


def score_jobs(part, b, g):
    tiles = range(QT) if part == "C" else (None,)
    return [("S", part, b, g, h, qt) for h in range(8) for qt in tiles]


def prob_units(part, b, g):
    if part == "A":
        return [[("U", part, b, g, 0, j) for j in range(4)] + [("PV", part, b, g, 0)]]
    per = range(0, 4, 2) if part == "B" else range(4)
    return [[("U", part, b, g, hh, j) for j in per] + [("PV", part, b, g, hh)] for hh in range(2)]


def interleave(a, b):
    out, i, j = [], 0, 0
    while i < len(a) or j < len(b):
        if j >= len(b) or (i < len(a) and i * len(b) <= j * len(a)):
            out.append(a[i])
            i += 1
        else:
            out.append(b[j])
            j += 1
    return out


def delay_pv(steps, by):
    out, held = [], []
    for s in steps:
        if s[0] == "PV":
            held.append([s, by])
            continue
        out.append(s)
        if s[0] == "U":
            for h in held:
                h[1] -= 1
            while held and held[0][1] <= 0:
                out.append(held.pop(0)[0])
    return out + [h[0] for h in held]


def max_steps(part, b, g):
    return score_jobs(part, b, g) + [("MS", part, b, g)]


def plan():
    def ys(part, b, g):
        return [s for grp in prob_units(part, b, g) for s in grp]

    def ffn(b):
        return [("GATE", b)] + [("F", b, e, t) for e in range(E) for t in range(QT)]

    post_a = [[("TY", "A", b), ("YT", b, 0), ("WO", b, 0), ("XT", b, 0), ("PROJ", b)] for b in range(B)]
    post_c = [[("TY", "B", b), ("TY", "C", b), ("YT", b, 1), ("WO", b, 1), ("XT", b, 1)] for b in range(B)]
    steps = []
    steps += max_steps("A", 0, 0) + [("W1", 0)] + [("MT", "A", 0, 0)]
    steps += max_steps("A", 0, 1) + [("W1", 1), ("MT", "A", 0, 1)]
    steps += interleave(max_steps("A", 1, 0), delay_pv(ys("A", 0, 0), 1)) + [("MT", "A", 1, 0)]
    steps += interleave(max_steps("A", 1, 1), ys("A", 0, 1)) + [("MT", "A", 1, 1)]
    steps += interleave(post_a[0], ys("A", 1, 0) + ys("A", 1, 1)[:4]) + ys("A", 1, 1)[4:]
    steps += interleave(post_a[1], max_steps("B", 0, 0)) + [("MT", "B", 0, 0)]
    steps += max_steps("B", 0, 1)
    steps += [("MT", "B", 0, 1)]
    steps += interleave(max_steps("C", 0, 0), delay_pv(ys("B", 0, 0) + ys("B", 0, 1), 1)) + [("MT", "C", 0, 0)]
    steps += interleave(max_steps("C", 0, 1) + [("MT", "C", 0, 1)] + max_steps("B", 1, 0), delay_pv(ys("C", 0, 0), 1)) + [("MT", "B", 1, 0)]
    steps += interleave(max_steps("B", 1, 1) + [("MT", "B", 1, 1)] + max_steps("C", 1, 0), delay_pv(ys("C", 0, 1), 1)) + [("MT", "C", 1, 0)]
    steps += interleave(max_steps("C", 1, 1), delay_pv(ys("B", 1, 0) + ys("B", 1, 1), 1)) + [("MT", "C", 1, 1)]
    steps += interleave(post_c[0] + ffn(0), delay_pv(ys("C", 1, 0) + ys("C", 1, 1), 1)) + [("OUT", 0)]
    steps += post_c[1] + ffn(1) + [("OUT", 1)]
    return steps


def build(nc, x, ctx_in, wts, out):
    steps = plan()
    mb_of = {s[1:4]: n for n, s in enumerate(s for s in steps if s[0] == "MS")}
    unit_of = {s[1:]: n for n, s in enumerate(s for s in steps if s[0] == "U")}
    unit_name = {n: u for u, n in unit_of.items()}
    pv_list = [s[1:] for s in steps if s[0] == "PV"]
    pv_of = {s: n for n, s in enumerate(pv_list)}
    unit_pv = {n: pv_of[u[:4]] for u, n in unit_of.items()}
    f_of = {s[1:]: n for n, s in enumerate(s for s in steps if s[0] == "F")}
    xt_of = {s[1:]: n for n, s in enumerate(s for s in steps if s[0] == "XT")}

    with ExitStack() as stack:
        def sb(name, shape, dt=F32):
            return stack.enter_context(nc.sbuf_tensor(name, shape, dt))

        def ps(name, shape):
            return stack.enter_context(nc.psum_tensor(name, shape, F32))

        def sem(name):
            return stack.enter_context(nc.semaphore(name))

        ident = sb("ident", [P, P])
        ident_bf = sb("ident_bf", [P, P], BF16)
        mask_q = sb("mask_q", [P, P], BF16)
        mask_k = sb("mask_k", [P, P], BF16)
        expert_no = sb("expert_no", [P, E])
        half_neg = sb("half_neg", [P, QT])
        bias_sel = sb("bias_sel", [3 * E, E, P], BF16)
        x_sb = sb("x_sb", [P, N // P, C])
        wg_nat = sb("wg_nat", [E, C])
        wx = sb("wx", [P, 5, C])
        wc = sb("wc", [CC, 2, C])
        bias_col = sb("bias_col", [P, 6])
        bias_row = sb("bias_row", [P, 6, C])
        w_a = sb("w_a", [P, C + 2 * D])
        w_T = sb("w_T", [P, 3 * C + E])
        w_oT, w_gT = w_T[:, 0:C], w_T[:, 3 * C:3 * C + E]
        w_ofT = w_T[:, C:3 * C].rearrange("p (i c) -> p i c", c=C)
        w1T = sb("w1T", [P, E, 2 * HF])
        xT = sb("xT", [P, N])
        x1T = x2T = xT
        q_stack = {p: sb(f"q_stack_{p}", [KROWS, H, N], BF16) for p in "AB"}
        q_stack["C"] = q_stack["A"]
        k_stack_a = sb("k_stack_a", [KROWS, N], BF16)
        k_stack_b = sb("k_stack_b", [KROWS, H, N], BF16)
        k_stack_c = sb("k_stack_c", [KROWS, H, B * TC], BF16)
        v_a = sb("v_a", [P, N // P, VW])
        v_b = sb("v_b", [P, N // P, H * VD + VW - VD])
        v_c = sb("v_c", [P, B * TC // P, H * VD + VW - VD])
        val_q = sb("val_q", [P, N])
        part_q = sb("part_q", [P, 3, N], BF16)
        part_qc = sb("part_qc", [P, 3, N], BF16)
        part_k = sb("part_k", [P, 3, N], BF16)
        b1_stack = sb("b1_stack", [3 * E, 2 * HF], BF16)
        NMB = len(mb_of)
        mneg = sb("mneg", [P, NMB, 3, 8])
        mpart = sb("mpart", [P, NMB, QT, 3, 8], BF16)
        mrow = sb("mrow", [24, NROW, T], BF16)
        probs = sb("probs", [P, NPT, 1024])
        wqk_nat = probs[:, 3, 0:4 * C].rearrange("p (n c) -> p n c", c=C)
        w1_nat = probs[:, NPT // 2:, :].rearrange("p a b -> p (a b)").rearrange("p (n c) -> p n c", c=C)
        y_sb = sb("y_sb", [P, 8, 512])
        val_c = y_sb[:, 0:2, :].rearrange("p a b -> p (a b)")
        part_c = y_sb[:, 2:5, :].bitcast(BF16)
        b1_part = y_sb[0:E, 5:7, :].rearrange("p a b -> p (a b)").bitcast(BF16)[:, 0:3 * 512].rearrange("p (r n) -> p r n", r=3)
        ysum = sb("ysum", [P, 32, 1])
        ytok = sb("ytok", [P, 2, QT * C])
        ctx_sb = ytok[:].rearrange("p a b -> p (a b)").rearrange("p (t c) -> p t c", c=CC)
        yT = sb("yT", [P, T])
        xpb = sb("xpb", [P, N // P, C])
        z = sb("z", [P, QT, C])
        stats = sb("stats", [P, QT, 6])
        mv = sb("mv", [P, QT, 2])
        rstd = sb("rstd", [P, 6, QT])
        x1 = sb("x1", [P, N // P, C])
        x2 = x1
        gate = sb("gate", [P, B, 11, QT, 8])
        gate_i = sb("gate_i", [P, B, QT, 8], U32)
        tanh_b = sb("tanh_b", [P, 4, HF])
        gated = sb("gated", [P, 2, HF])
        nat = tanh_b[:].rearrange("p a b -> p (a b)")
        wqkv_nat = nat[:, 0:3 * C].rearrange("p (a c) -> p a c", a=3)
        wo_nat = nat[:, 3 * C:4 * C]
        wof_nat = nat[:, 4 * C:4 * C + HF]
        b1_sb = gated[0:E].rearrange("p a b -> p (a b)")
        gsum = sb("gsum", [P, B, QT, HF])
        ctxT = gsum[0:CC].rearrange("p b t n -> p (b t n)")
        gT = sb("gT", [P, 512])
        val_k = gT
        val_qc = gated[:].rearrange("p a b -> p (a b)")
        fin = x_sb

        region = {"w0": ps("w0", [P, 512]), "w1": ps("w1", [P, 512]), "t0": ps("t0", [P, 1024]),
                  "t1": ps("t1", [P, 1024]), "y": ps("y", [P, 512]), "m": ps("m", [P, 512])}
        full = {r: sem(f"full_{r}") for r in region}
        free = {r: sem(f"free_{r}") for r in region}

        ld_x, ld_wa, ld_ctx, ld_wx, ld_w1, ld_rest, ld_bias, ld_brow, ld_b1 = map(
            sem, ("ld_x", "ld_wa", "ld_ctx", "ld_wx", "ld_w1", "ld_rest", "ld_bias", "ld_brow", "ld_b1"))
        ld_wck, s_wck, s_wqk = sem("ld_wck"), sem("wck_ordered"), sem("wqk_ordered")
        ld_wqk = sem("ld_wqk")
        s_ident, s_ident_bf, s_mask, s_small, s_sel = map(sem, ("ident_made", "ident_bf_made", "masks_made", "small_made", "sel_made"))
        cleared = {k: sem(f"cleared_{k}") for k in ("qA", "qB", "qC", "kA", "kB", "kC", "vA", "vB", "vC")}
        chain_pool, chain_dve, chain_act = sem("chain_pool"), sem("chain_dve"), sem("chain_act")
        s_bias = sem("bias_scaled")
        s_parts = {k: sem(f"parts_{k}") for k in ("qA", "kA", "qB0", "kB0", "qC0", "qB1", "kB1", "qC1", "kC", "b1")}
        s_stack = {k: sem(f"stack_{k}") for k in s_parts}
        s_mpart = sem("max_parts")
        s_shift = [sem(f"shift_{n}") for n in range(NMB)]
        s_pv = sem("pv_done")
        s_ytok, s_xres, s_var, s_rstd, s_xn = map(sem, ("y_normed", "residual_ready", "variance", "rstd", "x_normed"))
        s_lmax, s_gexp, s_comb, s_tanh, s_gated, s_fin, s_store = map(
            sem, ("gate_max", "gate_exp", "gate_comb", "tanh_done", "gated_sum", "fin_ready", "stored"))

        block = stack.enter_context(nc.Block())
        filled = {}
        fills = {r: 0 for r in region}

        def wait_full(eng, name):
            r, k = filled[name]
            eng.wait_ge(full[r], k + 1)
            return region[r]

        def emptied(ins, name):
            ins.then_inc(free[filled[name][0]], 1)

        def wait_emptied(eng, name):
            r, k = filled[name]
            eng.wait_ge(free[r], k + 1)

        def y_slot(part, b, g):
            return y_sb[:, {"A": 2 * b, "B": 4 - 4 * b, "C": 6 - 4 * b}[part] + g, :]

        def d_major(w, inverse=False):
            return w.rearrange("p (d h) -> p d h", d=D) if inverse else w.rearrange("p (h d) -> p d h", d=D)

        def head_values(v):
            return v[:, 0:H * VD].rearrange("p (h w) -> p h w", w=VD)[:, :, 0:D]

        def stack_key(part, b):
            return {"A": "kA", "B": f"kB{b}", "C": "kC"}[part]

        @block.tensor
        def _(pe):
            def take(r, name):
                if fills[r]:
                    pe.wait_ge(free[r], fills[r])
                filled[name] = (r, fills[r])
                fills[r] += 1
                return region[r]

            def give(ins, name):
                ins.then_inc(full[filled[name][0]], 1)

            turn = {"w": 0, "t": 0}

            def ring(kind, name):
                r = f"{kind}{turn[kind] % 2}"
                turn[kind] += 1
                return take(r, name)

            pe.wait_ge(s_ident, 1)
            pe.wait_ge(ld_x, 16)
            o = ring("t", "xT")
            for i in range(4):
                last = nc.tensor.transpose(o[:, i * P:(i + 1) * P], x_sb[:, i, :], ident[:])
            give(last, "xT")
            pe.wait_ge(ld_wa, 48)
            o = ring("t", "wa")
            nc.tensor.transpose(o[:, 0:C], wqkv_nat[:, 0, :], ident[:])
            nc.tensor.transpose(o[:, C:C + D], wqkv_nat[0:D, 1, :], ident[0:D, 0:D])
            last = nc.tensor.transpose(o[:, C + D:C + 2 * D], wqkv_nat[0:D, 2, :], ident[0:D, 0:D])
            give(last, "wa")
            wait_emptied(pe, "xT")
            wait_emptied(pe, "wa")
            o = ring("w", "qA")
            give(nc.tensor.matmul(o[:], w_a[:, 0:C], xT[:], start=True, stop=True), "qA")
            o = ring("w", "kA")
            give(nc.tensor.matmul(o[0:D, :], w_a[:, C:C + D], xT[:], start=True, stop=True), "kA")
            o = take("m", "vA")
            for i in range(4):
                last = nc.tensor.matmul(o[:, i * D:(i + 1) * D], xT[:, i * P:(i + 1) * P],
                                        w_a[:, C + D:C + 2 * D], start=True, stop=True)
            give(last, "vA")
            pe.wait_ge(ld_ctx, 32)
            o = ring("t", "ctxT")
            for i in range(8):
                last = nc.tensor.transpose(o[0:CC, i * P:(i + 1) * P], ctx_sb[:, i, :], ident[:])
            give(last, "ctxT")
            wait_emptied(pe, "ctxT")
            pe.wait_ge(s_wck, 1)
            o = ring("t", "kC")
            for i in range(2):
                last = nc.tensor.matmul(o[:, i * 512:(i + 1) * 512], wc[:, 0, :],
                                        ctxT[:, i * 512:(i + 1) * 512], start=True, stop=True)
            give(last, "kC")
            o = ring("t", "vC")
            for i in range(8):
                last = nc.tensor.matmul(o[:, i * P:(i + 1) * P], ctxT[:, i * P:(i + 1) * P],
                                        wc[:, 1, :], start=True, stop=True)
            give(last, "vC")
            pe.wait_ge(ld_rest, 48)
            o = take("y", "wT")
            nc.tensor.transpose(o[:, 0:C], wo_nat, ident[:])
            for i in range(2):
                nc.tensor.transpose(o[:, (i + 1) * C:(i + 2) * C], wof_nat[:, i * P:(i + 1) * P], ident[:])
            last = nc.tensor.transpose(o[:, 3 * C:3 * C + E], wg_nat[:], ident[0:E, 0:E])
            give(last, "wT")

            for s in steps:
                kind = s[0]
                if kind == "S":
                    _, part, b, g, h, qt = s
                    head = 8 * g + h
                    if h == 0 and not qt and g == 0:
                        pe.wait_ge(s_stack["qA" if part == "A" else f"q{part}{b}"], 96)
                        pe.wait_ge(s_stack[stack_key(part, b)], 96)
                        pe.wait_ge(s_ident_bf, 1)
                        pe.wait_ge(s_mask, 1)
                    o = ring("w", s)
                    q = q_stack[part]
                    q0 = b * T
                    if part == "A":
                        for i in range(QT):
                            last = nc.tensor.matmul(o[:, i * T:(i + 1) * T], q[:, head, q0 + i * P:q0 + (i + 1) * P],
                                                    k_stack_a[:, q0:q0 + T], start=True, stop=True)
                    elif part == "B":
                        nc.tensor.matmul(o[:, 0:P], q[:, head, q0:q0 + P], k_stack_b[:, head, q0:q0 + P],
                                         start=True, stop=False)
                        nc.tensor.matmul(o[:, 0:P], ident_bf[:], mask_q[:], start=False, stop=True)
                        nc.tensor.matmul(o[:, P:3 * P], q[:, head, q0 + P:q0 + T], k_stack_b[:, head, q0:q0 + T],
                                         start=True, stop=False)
                        last = nc.tensor.matmul(o[:, 2 * P:3 * P], ident_bf[:], mask_q[:], start=False, stop=True)
                    else:
                        last = nc.tensor.matmul(o[:], q[:, head, q0 + qt * P:q0 + (qt + 1) * P],
                                                k_stack_c[:, head, b * TC:(b + 1) * TC], start=True, stop=True)
                    give(last, s)
                elif kind == "MT":
                    mb = mb_of[s[1:4]]
                    pe.wait_ge(s_mpart, mb + 1)
                    o = take("m", s).bitcast(BF16)
                    for i in range(QT):
                        last = nc.tensor.transpose(o[0:24, i * P:(i + 1) * P],
                                                   mpart[:, mb, i, :, :].rearrange("p r h -> p (r h)"), ident_bf[:])
                    give(last, s)
                elif kind == "U":
                    _, part, b, g, hh, j = s
                    pe.wait_ge(s_shift[mb_of[(part, b, g)]], 16)
                    o = ring("t", s)
                    q = q_stack[part]
                    q0 = b * T
                    if part == "A":
                        for kt in range(2):
                            rhs = q[:, 8 * g + j:8 * g + j + 5:4, q0:q0 + T]
                            last = nc.tensor.matmul(o[:, kt * 512:(kt + 1) * 512],
                                                    k_stack_a[:, q0 + kt * P:q0 + (kt + 1) * P], rhs,
                                                    start=True, stop=True)
                    elif part == "B":
                        for i in range(2):
                            head = 8 * g + 4 * hh + j + i
                            c0 = i * 512
                            nc.tensor.matmul(o[:, c0:c0 + T], k_stack_b[:, head, q0:q0 + P], q[:, head, q0:q0 + T],
                                             start=True, stop=False)
                            nc.tensor.matmul(o[:, c0:c0 + P], ident_bf[:], mask_k[:], start=False, stop=True)
                            nc.tensor.matmul(o[:, c0 + T:c0 + T + P], k_stack_b[:, head, q0 + P:q0 + T],
                                             q[:, head, q0 + P:q0 + T], start=True, stop=False)
                            last = nc.tensor.matmul(o[:, c0 + T:c0 + T + P], ident_bf[:], mask_k[:],
                                                    start=False, stop=True)
                    else:
                        head = 8 * g + 4 * hh + j
                        for kt in range(4):
                            k0 = b * TC + kt * P
                            last = nc.tensor.matmul(o[:, kt * T:(kt + 1) * T], k_stack_c[:, head, k0:k0 + P],
                                                    q[:, head, q0:q0 + T], start=True, stop=True)
                    give(last, s)
                elif kind == "PV":
                    _, part, b, g, hh = s
                    units = [n for u, n in unit_of.items() if u[:4] == s[1:]]
                    for n in sorted(units)[-2:]:
                        wait_emptied(pe, ("U",) + unit_name[n])
                    if part == "A":
                        wait_emptied(pe, "vA")
                        o = take("y", s)
                        for kt in range(2):
                            for j in range(4):
                                pr = probs[:, unit_of[("A", b, g, 0, j)] % NPT, kt * 512:(kt + 1) * 512]
                                last = nc.tensor.matmul(o[32 * j:32 * j + VW, :], v_a[:, 2 * b + kt, :], pr,
                                                        start=(kt == 0), stop=(kt == 1), tile_position=(0, 32 * j))
                    else:
                        if hh == 0:
                            o = take("y", ("Y", part, b, g))
                            y_open = o
                        else:
                            o = y_open
                        if part == "B":
                            wait_emptied(pe, ("qcv", b))
                            for kt in range(2):
                                for j in range(4):
                                    head = 8 * g + 4 * hh + j
                                    u = unit_of[("B", b, g, hh, j // 2 * 2)] % NPT
                                    c0 = (j % 2) * 512 + kt * T
                                    n = T - kt * P
                                    last = nc.tensor.matmul(
                                        o[32 * j:32 * j + VW, hh * T + kt * P:(hh + 1) * T], v_b[:, 2 * b + kt, VD * head:VD * head + VW],
                                        probs[:, u, c0:c0 + n], start=(kt == 0), stop=(kt == 1), tile_position=(0, 32 * j))
                        else:
                            wait_emptied(pe, "vC")
                            for kt in range(4):
                                for j in range(4):
                                    head = 8 * g + 4 * hh + j
                                    u = unit_of[("C", b, g, hh, j)] % NPT
                                    last = nc.tensor.matmul(
                                        o[32 * j:32 * j + VW, hh * T:(hh + 1) * T], v_c[:, 4 * b + kt, VD * head:VD * head + VW],
                                        probs[:, u, kt * T:(kt + 1) * T], start=(kt == 0), stop=(kt == 3),
                                        tile_position=(0, 32 * j))
                    last.then_inc(s_pv, 1)
                    if part == "A":
                        filled[("Y", part, b, g)] = filled[s]
                elif kind == "TY":
                    _, part, b = s
                    o = ring("t", s)
                    wait_emptied(pe, ("Y", part, b, 1))
                    for qt in range(QT):
                        for g in range(2):
                            for hh in range(2):
                                c0 = qt * 512 + (2 * g + hh) * P
                                last = nc.tensor.transpose(o[:, c0:c0 + P],
                                                           y_slot(part, b, g)[:, hh * T + qt * P:hh * T + (qt + 1) * P],
                                                           ident[:])
                    give(last, s)
                elif kind == "YT":
                    if s[2]:
                        pe.wait_ge(s_ytok, s[1] + 1)
                    else:
                        wait_emptied(pe, ("TY", "A", s[1]))
                    o = take("m", s)
                    for i in range(QT):
                        last = nc.tensor.transpose(o[:, i * P:(i + 1) * P], ytok[:, 0, i * C:(i + 1) * C], ident[:])
                    give(last, s)
                elif kind == "WO":
                    _, b, cross = s
                    wait_emptied(pe, ("YT", b, cross))
                    if cross:
                        pe.wait_ge(ld_wx, 32)
                    else:
                        wait_emptied(pe, "wT")
                    o = take("m", s)
                    for i in range(QT):
                        last = nc.tensor.matmul(o[:, i * C:(i + 1) * C], yT[:, i * P:(i + 1) * P],
                                                wx[:, 4, :] if cross else w_oT, start=True, stop=True)
                    give(last, s)
                elif kind == "XT":
                    _, b, cross = s
                    pe.wait_ge(s_xn, xt_of[(b, cross)] + 1)
                    o = take("m", s)
                    src = x2 if cross else x1
                    for i in range(QT):
                        last = nc.tensor.transpose(o[:, i * P:(i + 1) * P], src[:, 2 * b + i, :], ident[:])
                    give(last, s)
                elif kind == "PROJ":
                    b = s[1]
                    wait_emptied(pe, ("XT", b, 0))
                    pe.wait_ge(ld_wx, 32)
                    pe.wait_ge(s_wqk, 1)
                    cols = slice(b * T, (b + 1) * T)
                    o = ring("w", ("qk", b))
                    nc.tensor.matmul(o[:, 0:T], wx[:, 0, :], x1T[:, cols], start=True, stop=True)
                    give(nc.tensor.matmul(o[:, T:2 * T], wx[:, 1, :], x1T[:, cols], start=True, stop=True), ("qk", b))
                    o = ring("w", ("qcv", b))
                    nc.tensor.matmul(o[:, 0:T], wx[:, 2, :], x1T[:, cols], start=True, stop=True)
                    for i in range(QT):
                        last = nc.tensor.matmul(o[:, T + i * C:T + (i + 1) * C],
                                                x1T[:, b * T + i * P:b * T + (i + 1) * P], wx[:, 3, :],
                                                start=True, stop=True)
                    give(last, ("qcv", b))
                elif kind == "W1":
                    pe.wait_ge(ld_w1, 16)
                    for n in range(4):
                        name = ("W1", s[1], n)
                        e, c = s[1] * 4 + n, 0
                        o = ring("t", name)
                        for c in range(4):
                            last = nc.tensor.transpose(o[:, c * P:(c + 1) * P], w1_nat[:, 4 * e + c, :], ident[:])
                        give(last, name)
                elif kind == "GATE":
                    b = s[1]
                    wait_emptied(pe, ("XT", b, 1))
                    wait_emptied(pe, "wT")
                    o = take("m", s)
                    for i in range(QT):
                        last = nc.tensor.matmul(o[:, i * E:(i + 1) * E], x2T[:, b * T + i * P:b * T + (i + 1) * P],
                                                w_gT, start=True, stop=True)
                    give(last, s)
                elif kind == "F":
                    _, b, e, t = s
                    if f_of[s[1:]] == 0:
                        wait_emptied(pe, ("W1", 1, 3))
                        pe.wait_ge(s_stack["b1"], 48)
                        pe.wait_ge(s_sel, 1)
                    o = ring("w", s)
                    nc.tensor.matmul(o[:], x2T[:, b * T + t * P:b * T + (t + 1) * P], w1T[:, e, :], start=True, stop=False)
                    last = nc.tensor.matmul(o[:], bias_sel[:, e, :], b1_stack[:], start=False, stop=True)
                    give(last, s)
                elif kind == "OUT":
                    b = s[1]
                    pe.wait_ge(s_gated, f_of[(b, E - 1, QT - 1)] + 1)
                    o = take("m", ("gT", b))
                    for i in range(QT):
                        for c in range(2):
                            last = nc.tensor.transpose(o[:, c * T + i * P:c * T + (i + 1) * P],
                                                       gsum[:, b, i, c * P:(c + 1) * P], ident[:])
                    give(last, ("gT", b))
                    wait_emptied(pe, ("gT", b))
                    o = take("m", s)
                    for i in range(QT):
                        for c in range(2):
                            last = nc.tensor.matmul(o[:, i * C:(i + 1) * C], gT[:, c * T + i * P:c * T + (i + 1) * P],
                                                    w_ofT[:, c, :], start=(c == 0), stop=(c == 1))
                    give(last, s)

        @block.vector
        def _(dve):
            V = nc.vector
            linked = [0]

            def link(ins):
                linked[0] += 1
                ins.then_inc(chain_dve, 1)
                dve.wait_ge(chain_dve, linked[0])

            def split(val, part, done):
                link(V.tensor_tensor(val, val, part(0), ALU.subtract))
                link(V.tensor_copy(part(1), val))
                V.tensor_tensor(part(2), val, part(1), ALU.subtract).then_inc(done, 1)

            def norm(zt, n, dst):
                V.bn_stats(stats[:, 0, :], zt[:, 0, :])
                link(V.bn_stats(stats[:, 1, :], zt[:, 1, :]))
                V.bn_aggr(mv[:, 0, :], stats[:, 0, :])
                V.bn_aggr(mv[:, 1, :], stats[:, 1, :]).then_inc(s_var, 1)
                dve.wait_ge(s_rstd, n + 1)
                for i in range(QT):
                    ins = V.tensor_scalar(dst[:, i, :], zt[:, i, :], mv[:, i, 0:1], rstd[:, n, i:i + 1],
                                          ALU.subtract, ALU.mult)
                return ins

            V.memset(q_stack["A"][:], 0.0).then_inc(cleared["qA"], 1)
            o = wait_full(dve, "xT")
            emptied(V.tensor_copy(xT[:], o[:, 0:512]), "xT")
            dve.wait_ge(ld_bias, 80)
            V.tensor_scalar(bias_col[:, 0:3], bias_col[:, 0:3], SCALE, None, ALU.mult).then_inc(s_bias, 1)
            wait_emptied(dve, "qA")
            split(val_q[:], lambda r: part_q[:, r, :], s_parts["qA"])
            wait_emptied(dve, "kA")
            split(val_k[0:D, :], lambda r: part_k[0:D, r, :], s_parts["kA"])
            dve.wait_ge(ld_brow, 96)
            dve.wait_ge(cleared["vA"], 1)
            o = wait_full(dve, "vA")
            ins = V.tensor_tensor(v_a[:, :, 0:D], o[:, 0:4 * D].rearrange("p (i d) -> p i d", d=D),
                                  bias_row[:, 0:1, 0:D].to_broadcast([P, 4, D]), ALU.add)
            emptied(ins, "vA")
            dve.wait_ge(cleared["vC"], 1)
            o = wait_full(dve, "vC")
            for i in range(8):
                ins = V.tensor_tensor(head_values(v_c[:, i, :]), o[:, i * P:(i + 1) * P].rearrange("p (h d) -> p h d", d=D),
                                      bias_row[:, 2, :].rearrange("p (h d) -> p h d", d=D), ALU.add)
            emptied(ins, "vC")
            dve.wait_ge(ld_b1, 16)
            link(V.tensor_copy(b1_part[:, 0, :], b1_sb))
            split(b1_sb, lambda r: b1_part[:, r, :], s_parts["b1"])

            n_norm = 0
            for s in steps:
                kind = s[0]
                if kind == "S":
                    _, part, b, g, h, qt = s
                    mb = mb_of[(part, b, g)]
                    o = wait_full(dve, s)
                    if part == "A":
                        dst, src = mneg[:, mb, 0:2, h], o[:].rearrange("p (a k) -> p a k", a=2)
                    elif part == "B":
                        dst, src = mneg[:, mb, :, h], o[:, 0:3 * P].rearrange("p (a k) -> p a k", a=3)
                    else:
                        dst, src = mneg[:, mb, qt, h:h + 1], o[:]
                    emptied(V.tensor_reduce(out=dst, in_=src, axis=AX.X, op=ALU.max, negate=True), s)
                    last_s = s
                elif kind == "MS":
                    mb = mb_of[s[1:4]]
                    wait_emptied(dve, last_s)
                    if s[1] == "B":
                        link(V.tensor_tensor(mneg[:, mb, 1, :], mneg[:, mb, 1, :], mneg[:, mb, 2, :], ALU.min))
                    link(V.tensor_copy(mpart[:, mb, :, 0, :], mneg[:, mb, 0:2, :]))
                    split(mneg[:, mb, 0:2, :], lambda r: mpart[:, mb, :, r, :], s_mpart)
                elif kind == "MT":
                    mb = mb_of[s[1:4]]
                    if mb >= NROW:
                        dve.wait_ge(s_shift[mb - NROW], 16)
                    o = wait_full(dve, s).bitcast(BF16)
                    emptied(V.tensor_copy(mrow[:, mb % NROW, :], o[0:24, 0:T]), s)
                elif kind == "PV":
                    part, b, g, hh = s[1:]
                    if part == "A" or hh == 1:
                        name = ("Y", part, b, g)
                        dve.wait_ge(s_pv, pv_of[s[1:]] + 1)
                        dve.wait_ge(s_stack["kC"], 96)
                        dve.wait_ge(s_stack["b1"], 48)
                        emptied(V.tensor_copy(y_slot(part, b, g), region["y"][:]), name)
                elif kind == "TY":
                    _, part, b = s
                    o = wait_full(dve, s).rearrange("p (n w) -> p n w", w=VW)
                    link(V.reciprocal(ysum[:], o[:, :, D:D + 1]))
                    dst = ytok[:, 1 if part == "C" else 0, :].rearrange("p (n d) -> p n d", d=D)
                    emptied(V.tensor_tensor(dst, o[:, :, 0:D], ysum[:].to_broadcast([P, 32, D]), ALU.mult), s)
                    wait_emptied(dve, s)
                    if part == "C":
                        V.tensor_tensor(ytok[:, 0, :], ytok[:, 0, :], ytok[:, 1, :], ALU.add).then_inc(s_ytok, 1)
                elif kind == "YT":
                    o = wait_full(dve, s)
                    emptied(V.tensor_copy(yT[:], o[:, 0:T]), s)
                elif kind == "WO":
                    _, b, cross = s
                    dve.wait_ge(s_xres, 1 if not cross else 2 + b)
                    o = wait_full(dve, s)
                    ins = V.tensor_tensor(z[:], o[:, 0:T].rearrange("p (i c) -> p i c", c=C),
                                          xpb[:, 2 * b:2 * b + 2, :], ALU.add)
                    emptied(ins, s)
                    wait_emptied(dve, s)
                    norm(z, n_norm, (x2 if cross else x1)[:, 2 * b:2 * b + 2, :]).then_inc(s_xn, 1)
                    n_norm += 1
                elif kind == "XT":
                    _, b, cross = s
                    o = wait_full(dve, s)
                    emptied(V.tensor_copy((x2T if cross else x1T)[:, b * T:(b + 1) * T], o[:, 0:T]), s)
                elif kind == "PROJ":
                    b = s[1]
                    cols = slice(b * T, (b + 1) * T)
                    wait_emptied(dve, ("qk", b))
                    split(val_q[:, cols], lambda r: part_q[:, r, cols], s_parts[f"qB{b}"])
                    o = wait_full(dve, ("qcv", b))
                    link(V.tensor_scalar(val_qc[:, cols], o[:, 0:T], SCALE, bias_col[:, 2:3], ALU.mult, ALU.add))
                    dve.wait_ge(cleared["vB"], 1)
                    for i in range(QT):
                        ins = V.tensor_tensor(head_values(v_b[:, 2 * b + i, :]),
                                              o[:, T + i * C:T + (i + 1) * C].rearrange("p (h d) -> p h d", d=D),
                                              bias_row[:, 1, :].rearrange("p (h d) -> p h d", d=D), ALU.add)
                    emptied(ins, ("qcv", b))
                    link(V.tensor_copy(part_qc[:, 0, cols], val_qc[:, cols]))
                    split(val_qc[:, cols], lambda r: part_qc[:, r, cols], s_parts[f"qC{b}"])
                elif kind == "GATE":
                    b = s[1]
                    t = {k: gate[:, b, n, :, :] for n, k in enumerate(
                        ("logit", "stat", "small", "exp", "score", "top", "index", "weight", "one0", "one1", "comb"))}
                    small = lambda n: t["small"][:, :, n:n + 1]
                    o = wait_full(dve, s)
                    emptied(V.tensor_copy(t["logit"], o[:, 0:QT * E].rearrange("p (i e) -> p i e", e=E)), s)
                    wait_emptied(dve, s)
                    V.tensor_reduce(out=t["stat"][:, :, 0], in_=t["logit"], axis=AX.X, op=ALU.max,
                                    negate=True).then_inc(s_lmax, 1)
                    dve.wait_ge(s_gexp, b + 1)
                    link(V.reciprocal(small(0), t["stat"][:, :, 1:2]))
                    link(V.tensor_tensor(t["score"], t["exp"], small(0).to_broadcast([P, QT, E]), ALU.mult))
                    for i in range(QT):
                        link(V.max(out=t["top"][:, i, :], in_=t["score"][:, i, :]))
                        link(V.max_index(gate_i[:, b, i, :], t["top"][:, i, :], t["score"][:, i, :]))
                    link(V.tensor_copy(t["index"], gate_i[:, b]))
                    link(V.tensor_tensor(small(1), t["top"][:, :, 0:1], t["top"][:, :, 1:2], ALU.add))
                    link(V.tensor_scalar(small(2), small(1), EPS_TOP, None, ALU.add))
                    link(V.reciprocal(small(3), small(2)))
                    link(V.tensor_tensor(t["weight"][:, :, 0:2], t["top"][:, :, 0:2],
                                         small(3).to_broadcast([P, QT, 2]), ALU.mult))
                    link(V.tensor_tensor(small(4), t["weight"][:, :, 0:1], t["weight"][:, :, 1:2], ALU.add))
                    link(V.tensor_scalar(t["weight"][:, :, 2:4], t["weight"][:, :, 0:2], 0.5, None, ALU.mult))
                    for i in range(QT):
                        for k in range(2):
                            link(V.tensor_scalar(t[f"one{k}"][:, i, :], expert_no[:], t["index"][:, i, k:k + 1],
                                                 t["weight"][:, i, 2 + k:3 + k], ALU.is_equal, ALU.mult))
                    link(V.tensor_tensor(t["comb"], t["one0"], t["one1"], ALU.add))
                    for i in range(QT):
                        link(V.scalar_tensor_tensor(out=xpb[:, 2 * b + i, :], in0=bias_row[:, 5, :],
                                                    scalar=t["small"][:, i, 4:5], in1=x2[:, 2 * b + i, :],
                                                    op0=ALU.mult, op1=ALU.add))
                elif kind == "F":
                    _, b, e, t = s
                    n = f_of[s[1:]]
                    dve.wait_ge(s_tanh, n + 1)
                    o = wait_full(dve, s)
                    product = gated[:, n % 2, :]
                    emptied(V.scalar_tensor_tensor(out=product, in0=tanh_b[:, n % 4, :], scalar=1.0, in1=o[:, 0:HF],
                                                   op0=ALU.add, op1=ALU.mult), s)
                    wait_emptied(dve, s)
                    dst = gsum[:, b, t, :]
                    weight = gate[:, b, 10, t, e:e + 1]
                    if e == 0:
                        ins = V.tensor_scalar(dst, product, weight, None, ALU.mult)
                    else:
                        dve.wait_ge(s_gated, n - 1)
                        ins = V.scalar_tensor_tensor(out=dst, in0=product, scalar=weight, in1=dst,
                                                     op0=ALU.mult, op1=ALU.add)
                    ins.then_inc(s_gated, 1)
                elif kind == "OUT":
                    b = s[1]
                    o = wait_full(dve, ("gT", b))
                    emptied(V.tensor_copy(gT[:], o[:]), ("gT", b))
                    o = wait_full(dve, s)
                    ins = V.tensor_tensor(z[:], o[:, 0:T].rearrange("p (i c) -> p i c", c=C),
                                          xpb[:, 2 * b:2 * b + 2, :], ALU.add)
                    emptied(ins, s)
                    wait_emptied(dve, s)
                    norm(z, n_norm, fin[:, 2 * b:2 * b + 2, :]).then_inc(s_fin, 1)
                    n_norm += 1

        @block.scalar
        def _(act):
            A = nc.scalar
            for t, name in enumerate(("L0_attn_bq", "L0_xattn_bq", "L0_xattn_bcq", "L0_xattn_bk", "L0_xattn_bck")):
                act.dma_start(bias_col[:, t:t + 1], wts[name].rearrange("(h d) -> d h", d=D),
                              allow_slow_non_contiguous=True).then_inc(ld_bias, 16)
            act.dma_start(wqk_nat[0:CC, 3, :], wts["L0_xattn_Wck"]).then_inc(ld_wck, 16)
            act.dma_start(wc[:, 1, :], wts["L0_xattn_Wcv"]).then_inc(ld_ctx, 16)

            o = wait_full(act, "wa")
            A.activation(d_major(w_a[:, 0:C], inverse=True), d_major(o[:, 0:C]), ACT.Copy)
            emptied(A.activation(w_a[:, C:], o[:, C:C + 2 * D], ACT.Copy), "wa")
            act.wait_ge(s_bias, 1)
            o = wait_full(act, "qA")
            A.activation(val_q[:], o[:], ACT.Identity, bias=bias_col[:, 0:1], scale=SCALE)
            emptied(A.activation(part_q[:, 0, :], o[:], ACT.Identity, bias=bias_col[:, 0:1], scale=SCALE), "qA")
            o = wait_full(act, "kA")
            A.activation(val_k[0:D, :], o[0:D, :], ACT.Copy)
            emptied(A.activation(part_k[0:D, 0, :], o[0:D, :], ACT.Copy), "kA")
            o = wait_full(act, "ctxT")
            emptied(A.activation(ctxT, o[0:CC, :], ACT.Copy), "ctxT")
            o = wait_full(act, "kC")
            A.activation(val_c, o[:], ACT.Identity, bias=bias_col[:, 4:5])
            emptied(A.activation(part_c[:, 0, :], o[:], ACT.Identity, bias=bias_col[:, 4:5]), "kC")
            o = wait_full(act, "wT")
            emptied(A.activation(w_T[:], o[:, 0:3 * C + E], ACT.Copy), "wT")

            for s in steps:
                kind = s[0]
                if kind == "W1":
                    for n in range(4):
                        name = ("W1", s[1], n)
                        o = wait_full(act, name)
                        emptied(A.activation(w1T[:, 4 * s[1] + n, :], o[:, 0:512], ACT.Copy), name)
                elif kind == "U":
                    n = unit_of[s[1:]]
                    if n >= NPT:
                        act.wait_ge(s_pv, unit_pv[n - NPT] + 1)
                    if n == 3:
                        act.wait_ge(s_wqk, 1)
                    o = wait_full(act, s)
                    dst = probs[:, n % NPT, :]
                    if s[1] == "B":
                        ins = A.activation(dst.rearrange("p (i c) -> p i c", i=2)[:, :, 0:T + P],
                                           o[:].rearrange("p (i c) -> p i c", i=2)[:, :, 0:T + P], ACT.Exp)
                    else:
                        ins = A.activation(dst, o[:], ACT.Exp)
                    emptied(ins, s)
                elif kind == "PROJ":
                    b = s[1]
                    cols = slice(b * T, (b + 1) * T)
                    name = ("qk", b)
                    o = wait_full(act, name)
                    act.wait_ge(s_stack["qA"], 96)
                    A.activation(val_q[:, cols], o[:, 0:T], ACT.Identity, bias=bias_col[:, 1:2], scale=SCALE)
                    A.activation(part_q[:, 0, cols], o[:, 0:T], ACT.Identity, bias=bias_col[:, 1:2], scale=SCALE)
                    act.wait_ge(s_stack["kA"], 96)
                    A.activation(val_k[:, cols], o[:, T:2 * T], ACT.Identity, bias=bias_col[:, 3:4])
                    emptied(A.activation(part_k[:, 0, cols], o[:, T:2 * T], ACT.Identity, bias=bias_col[:, 3:4]), name)
                elif kind == "GATE":
                    b = s[1]
                    act.wait_ge(s_lmax, b + 1)
                    for i in range(QT):
                        ins = A.activation(gate[:, b, 3, i, :], gate[:, b, 0, i, :], ACT.Exp,
                                           bias=gate[:, b, 1, i, 0:1], accum_out=gate[:, b, 1, i, 1:2])
                    ins.then_inc(s_gexp, 1)
                elif kind == "F":
                    n = f_of[s[1:]]
                    if n >= 4:
                        act.wait_ge(s_gated, n - 3)
                    o = wait_full(act, s)
                    A.activation(tanh_b[:, n % 4, :], o[:, HF:2 * HF], ACT.Tanh, scale=0.5).then_inc(s_tanh, 1)

        @block.gpsimd
        def _(pool):
            G = nc.gpsimd
            linked = [0]

            def link(ins):
                linked[0] += 1
                ins.then_inc(chain_pool, 1)
                pool.wait_ge(chain_pool, linked[0])

            def split(val, part, done):
                link(G.tensor_tensor(val, val, part(0), ALU.subtract))
                link(G.tensor_copy(part(1), val))
                G.tensor_tensor(part(2), val, part(1), ALU.subtract).then_inc(done, 1)

            link(G.memset(ident[:], 0.0))
            G.affine_select(out=ident[:], in_=ident[:], compare_op=ALU.not_equal, fill=1.0, base=0,
                            pattern=[[-1, P]], channel_multiplier=1).then_inc(s_ident, 1)
            G.memset(k_stack_a[:], 1.0).then_inc(cleared["kA"], 1)
            G.memset(v_a[:], 1.0).then_inc(cleared["vA"], 1)
            link(G.memset(ident_bf[:], 0.0))
            G.affine_select(out=ident_bf[:], in_=ident_bf[:], compare_op=ALU.not_equal, fill=1.0, base=0,
                            pattern=[[-1, P]], channel_multiplier=1).then_inc(s_ident_bf, 1)
            G.memset(mask_q[:], 0.0)
            link(G.memset(mask_k[:], 0.0))
            G.affine_select(out=mask_q[:], in_=mask_q[:], compare_op=ALU.is_ge, fill=NEG, base=0,
                            pattern=[[-1, P]], channel_multiplier=1)
            G.affine_select(out=mask_k[:], in_=mask_k[:], compare_op=ALU.is_ge, fill=NEG, base=0,
                            pattern=[[1, P]], channel_multiplier=-1).then_inc(s_mask, 1)
            G.memset(half_neg[:], -0.5)
            for e in range(E):
                ins = G.memset(expert_no[:, e:e + 1], float(e))
            ins.then_inc(s_small, 1)
            pool.wait_ge(ld_brow, 96)
            pool.wait_ge(ld_x, 16)
            for i in range(N // P):
                ins = G.tensor_tensor(xpb[:, i, :], x_sb[:, i, :], bias_row[:, 3, :], ALU.add)
            ins.then_inc(s_xres, 1)
            pool.wait_ge(ld_wck, 16)
            G.tensor_copy(d_major(wc[:, 0, :], inverse=True), d_major(wqk_nat[0:CC, 3, :])).then_inc(s_wck, 1)
            G.memset(v_c[:], 1.0).then_inc(cleared["vC"], 1)
            pool.wait_ge(ld_wqk, 48)
            for t in range(3):
                ins = G.tensor_copy(d_major(wx[:, t, :], inverse=True), d_major(wqk_nat[:, t, :]))
            ins.then_inc(s_wqk, 1)
            wait_emptied(pool, "kC")
            split(val_c, lambda r: part_c[:, r, :], s_parts["kC"])
            G.memset(k_stack_c[:], 1.0).then_inc(cleared["kC"], 1)
            G.memset(q_stack["B"][:], 0.0).then_inc(cleared["qB"], 1)
            G.memset(k_stack_b[:], 1.0).then_inc(cleared["kB"], 1)
            G.memset(v_b[:], 1.0).then_inc(cleared["vB"], 1)
            link(G.memset(bias_sel[:], 0.0))
            for r in range(3):
                ins = G.affine_select(out=bias_sel[:], in_=bias_sel[:], compare_op=ALU.not_equal, fill=1.0,
                                      base=-8 * r, pattern=[[-1, E], [0, P]], channel_multiplier=1)
                if r < 2:
                    link(ins)
            ins.then_inc(s_sel, 1)

            n_norm = 0
            for s in steps:
                kind = s[0]
                if kind in ("WO", "OUT"):
                    pool.wait_ge(s_var, n_norm + 1)
                    link(G.tensor_scalar(rstd[:, n_norm, :], mv[:, :, 1], EPS_LN, None, ALU.add))
                    G.tensor_tensor(rstd[:, n_norm, :], rstd[:, n_norm, :], half_neg[:], ALU.pow).then_inc(s_rstd, 1)
                    n_norm += 1
                elif kind == "XT" and not s[2]:
                    b = s[1]
                    pool.wait_ge(s_xn, xt_of[(b, 0)] + 1)
                    for i in range(QT):
                        ins = G.tensor_tensor(xpb[:, 2 * b + i, :], x1[:, 2 * b + i, :], bias_row[:, 4, :], ALU.add)
                    ins.then_inc(s_xres, 1)
                elif kind == "PROJ":
                    b = s[1]
                    cols = slice(b * T, (b + 1) * T)
                    wait_emptied(pool, ("qk", b))
                    split(val_k[:, cols], lambda r: part_k[:, r, cols], s_parts[f"kB{b}"])
                    pool.wait_ge(s_pv, pv_of[("A", b, 1, 0)] + 1)
                    pool.wait_ge(s_parts[f"kB{b}"], 1)
                    G.memset(q_stack["C"][2 * 32:KROWS, :, cols], 0.0).then_inc(cleared["qC"], 1)
                    pool.wait_ge(cleared["qC"], b + 1)

        @block.sync
        def _(sp):
            sp.dma_start(x_sb[:], x.rearrange("b (t p) c -> p (b t) c", p=P)).then_inc(ld_x, 16)
            sp.dma_start(wqkv_nat[:, 0, :], wts["L0_attn_Wq"]).then_inc(ld_wa, 16)
            sp.dma_start(wqkv_nat[0:D, 1, :], wts["L0_attn_Wk"]).then_inc(ld_wa, 16)
            sp.dma_start(wqkv_nat[0:D, 2, :], wts["L0_attn_Wv"]).then_inc(ld_wa, 16)
            sp.dma_start(ctx_sb, ctx_in.rearrange("b (t p) c -> p (b t) c", p=P)).then_inc(ld_ctx, 16)
            sp.dma_start(bias_row[:, 0, 0:D], wts["L0_attn_bv"].partition_broadcast(P)).then_inc(ld_brow, 16)
            for t, name in ((1, "L0_xattn_bv"), (2, "L0_xattn_bcv"), (3, "L0_attn_bo"), (4, "L0_xattn_bp"), (5, "L0_ffn_bo")):
                sp.dma_start(bias_row[:, t, :], wts[name].partition_broadcast(P)).then_inc(ld_brow, 16)
            sp.dma_start(wo_nat, wts["L0_attn_Wo"]).then_inc(ld_rest, 16)
            sp.dma_start(wof_nat, wts["L0_ffn_Wo"]).then_inc(ld_rest, 16)
            sp.dma_start(wg_nat[:], wts["L0_ffn_Wg"]).then_inc(ld_rest, 16)
            sp.dma_start(b1_sb, wts["L0_ffn_b1"]).then_inc(ld_b1, 16)

            def make_stack(dst, terms, parts, key):
                sp.wait_ge(s_parts[key], 1)
                sp.wait_ge(cleared[key[:2]], 2 if key == "qC1" else 1)
                for r, p in enumerate(terms):
                    sp.dma_start(dst(r), parts(p)).then_inc(s_stack[key], 16)

            make_stack(lambda r: q_stack["A"][8 * r:8 * r + 8, :, :], Q_TERMS,
                       lambda p: part_q[:, p, :], "qA")
            make_stack(lambda r: k_stack_a[8 * r:8 * r + 8, :], K_TERMS,
                       lambda p: part_k[0:D, p, :], "kA")
            sp.dma_start(w1_nat, wts["L0_ffn_W1"].rearrange("e (c p) k -> p (e c) k", p=P)).then_inc(ld_w1, 16)
            for t, name in enumerate(("Wq", "Wk", "Wcq")):
                sp.dma_start(wqk_nat[:, t, :], wts[f"L0_xattn_{name}"]).then_inc(ld_wqk, 16)
            for t, name in enumerate(("Wv", "Wp")):
                sp.dma_start(wx[:, 3 + t, :], wts[f"L0_xattn_{name}"]).then_inc(ld_wx, 16)

            for s in steps:
                kind = s[0]
                if kind == "MT":
                    _, part, b, g = s
                    mb = mb_of[s[1:4]]
                    wait_emptied(sp, s)
                    sp.dma_start(q_stack[part][MROW:MROW + 3, 8 * g:8 * g + 8, b * T:(b + 1) * T],
                                 mrow[:, mb % NROW, :]).then_inc(s_shift[mb], 16)
                elif kind == "W1" and s[1] == 1:
                    make_stack(lambda r: k_stack_c[8 * r:8 * r + 8, :, :], K_TERMS,
                               lambda p: part_c[:, p, :], "kC")
                    sp.wait_ge(s_parts["b1"], 1)
                    for r in range(3):
                        sp.dma_start(b1_stack[E * r:E * r + E, :], b1_part[:, r, :]).then_inc(s_stack["b1"], 16)
                elif kind == "PROJ":
                    b = s[1]
                    cols = slice(b * T, (b + 1) * T)
                    make_stack(lambda r: q_stack["B"][8 * r:8 * r + 8, :, cols], Q_TERMS,
                               lambda p: part_q[:, p, cols], f"qB{b}")
                    make_stack(lambda r: k_stack_b[8 * r:8 * r + 8, :, cols], K_TERMS,
                               lambda p: part_k[:, p, cols], f"kB{b}")
                    make_stack(lambda r: q_stack["C"][8 * r:8 * r + 8, :, cols], Q_TERMS,
                               lambda p: part_qc[:, p, cols], f"qC{b}")
                elif kind == "OUT":
                    b = s[1]
                    sp.wait_ge(s_fin, b + 1)
                    sp.dma_start(out[b].rearrange("(t p) c -> p t c", p=P), fin[:, 2 * b:2 * b + 2, :]).then_inc(s_store, 16)
            sp.wait_ge(s_store, 16 * B)


def kernel(**inputs):
    import numpy as _np
    import concourse.bacc as _bacc
    from concourse import mybir as _mybir
    from concourse.bass_utils import run_bass_kernel_spmd as _run

    nc = _bacc.Bacc("TRN2", target_bir_lowering=False, num_devices=1)
    arrays, aps = {}, {}
    for name, a in inputs.items():
        a = _np.ascontiguousarray(a)
        arrays[f"in_{name}"] = a
        aps[name] = nc.dram_tensor(f"in_{name}", a.shape, _mybir.dt.from_np(a.dtype), kind="ExternalInput").ap()
    out = nc.dram_tensor("out_0", (B, T, C), _mybir.dt.float32, kind="ExternalOutput").ap()
    build(nc, aps.pop("x"), aps.pop("ctx_512"), aps, out)
    r = _run(nc, [arrays], core_ids=[0])
    return r.results[0]["out_0"]
```

```python
from contextlib import ExitStack

import numpy as np

import concourse.bass as bass
from concourse import mybir

F32 = mybir.dt.float32
BF16 = mybir.dt.bfloat16
U32 = mybir.dt.uint32
ALU = mybir.AluOpType
ACT = mybir.ActivationFunctionType
AX = mybir.AxisListType

P = 128
B, T, C, H, D = 2, 256, 128, 16, 8
TC, CC = 512, 64
E, HF = 8, 256
N = B * T
QT = T // P
SCALE = float(D) ** -0.5
EPS_LN = 1e-5
EPS_TOP = 1e-9
NEG = -1.0e30
ONES = float(np.uint32(0x3F803F80).view(np.float32))
KROWS = 128
MROW = 64
VD = D + 1
VW = 32
TERMS = ((0, 0, 0), (8, 1, 0), (16, 2, 0), (32, 0, 1), (40, 1, 1), (96, 0, 2))
STACKED = 16 * len(TERMS)
NPT = 8
NROW = 4


COSTS = {"SA": (0.3, 0.6), "SB": (0.22, 0.47), "SC": (0.22, 0.6), "MS": (0.0, 0.9), "MT": (0.12, 0.3),
         "UA": (0.6, 0.95), "UB": (0.5, 0.75), "UC": (0.5, 0.95), "PA": (0.8, 0.5), "PB": (0.3, 0.5), "PC": (0.3, 0.5),
         "TY": (0.9, 0.8), "YT": (0.3, 0.4), "WO": (0.4, 0.9), "LN": (0.0, 0.6), "XT": (0.4, 0.4), "PROJ": (2.2, 3.0),
         "VC": (1.7, 0.8), "GATE": (0.2, 6.0), "F": (1.1, 0.75), "OUT": (1.0, 3.0)}
SHIFT_US, STACK_US = 3.0, 5.0


def plan():
    groups = [(p, b, g) for b in range(B) for p in "A" for g in range(2)]
    groups += [(p, b, g) for b in range(B) for p in "BC" for g in range(2)]
    scores, shifts, probs, values = [], [], [], []
    for p, b, g in groups:
        tiles = range(QT) if p == "C" else (None,)
        scores += [("S", p, b, g, h, qt) for h in range(8) for qt in tiles] + [("MS", p, b, g)]
        shifts += [("MT", p, b, g)]
        for hh in range(1 if p == "A" else 2):
            probs += [("U", p, b, g, hh, j) for j in range(0, 4, 2 if p == "B" else 1)]
            values += [("PV", p, b, g, hh, kt) for kt in range(4 if p == "C" else 2)]
    posts = [[("TY", "A", b), ("YT", b, 0), ("WO", b, 0), ("LN", b, 0), ("XT", b, 0), ("PROJ", b)] for b in range(B)]
    ends = [[("TY", "B", b), ("TY", "C", b), ("YT", b, 1), ("WO", b, 1), ("LN", b, 1), ("XT", b, 1), ("GATE", b)]
            + [("F", b, e, t) for e in range(E) for t in range(QT)] + [("OUT", b)] for b in range(B)]
    streams = [posts[0], posts[1], ends[0], ends[1], shifts, probs, values, scores, [("VC", 0), ("VC", 1)]]
    last_kt = {"A": 1, "B": 1, "C": 3}
    opens = {("PV", p, b, g, 0, 0) for p, b, g in groups}
    closes = {("PV", p, b, g, 0 if p == "A" else 1, last_kt[p]) for p, b, g in groups}

    def needs(s):
        k = s[0]
        if k == "S" and s[1] != "A":
            return [(("PROJ", s[2]), STACK_US)]
        if k == "MT":
            return [(("MS",) + s[1:], 0.2)]
        if k == "U":
            n = probs.index(s) - NPT
            ring = [(("PV",) + probs[n][1:5] + (last_kt[probs[n][1]],), 0.0)] if n >= 0 else []
            return ring + [(("MT",) + s[1:4], SHIFT_US)]
        if s == ("WO", 0, 0):
            return [(("VC", 1), 0.0)]
        if k == "PV":
            return [(u, 0.1) for u in probs if u[:5] == ("U",) + s[1:5]]
        if k == "TY":
            part, b = s[1:]
            return [(("PV", part, b, 1, 0 if part == "A" else 1, last_kt[part]), 0.2)]
        return []

    region = {"S": "w", "F": "w", "PROJ": "w", "U": "t", "TY": "t", "VC": "t", "MT": "m", "YT": "m", "WO": "m", "XT": "m",
              "GATE": "m", "OUT": "m"}
    reader = {"U": "act", "PV": "act"}
    done, free_at, used = {}, {"pe": 0.0, "dve": 0.0, "act": 0.0}, {"w": [0.0, 0.0], "t": [0.0, 0.0], "m": [0.0], "y": [0.0]}
    last_of = [0.0] * len(streams)
    at, out = [0] * len(streams), []

    def start(n, s):
        if s[0] in ("YT", "OUT") and len({d for d in done if d[0] == "YT"}) > len({d for d in done if d[0] == "LN"}):
            return None
        need = needs(s)
        if any(d not in done for d, _ in need):
            return None
        t = max([free_at["pe"]] + [done[d] + lag for d, lag in need])
        if s[0] in ("YT", "WO", "XT", "PROJ", "GATE", "OUT") or s[0] == "F" and s[2:] == (0, 0):
            t = max(t, last_of[n])
        if s[0] == "LN":
            t = max(t, last_of[n] + 0.9 - 0.1)
        r = "y" if s in opens else region.get(s[0])
        return max(t, used[r][0]) if r else t

    def urgency(s, t):
        if s[0] in ("S", "MS"):
            return 0.8 if free_at["dve"] - t < 0.8 else -0.4
        if s[0] == "U":
            return 0.6 if free_at["act"] - t < 0.6 else 0.0
        return {"PV": 0.0, "F": -0.3, "VC": -1.5}.get(s[0], 1.0)

    while any(at[n] < len(q) for n, q in enumerate(streams)):
        best = None
        for n, q in enumerate(streams):
            if at[n] == len(q):
                continue
            t = start(n, q[at[n]])
            if t is None:
                continue
            rank = t - urgency(q[at[n]], t)
            if best is None or rank < best[0] - 0.01:
                best = (rank, t, n)
        _, t, n = best
        s = streams[n][at[n]]
        at[n] += 1
        key = {"S": "S", "U": "U", "PV": "P"}.get(s[0])
        pe, rest = COSTS[key + s[1] if key else s[0]]
        if pe:
            free_at["pe"] = t + pe
        eng = reader.get(s[0], "dve")
        end = t + pe
        if s[0] != "PV" or s in closes:
            end = max(end, free_at[eng]) + rest
            free_at[eng] = end
        r = "y" if s in closes else region.get(s[0])
        if r:
            used[r] = used[r][1:] + [end]
        done[s] = last_of[n] = end
        out.append(s)
    return out


def build(nc, packs, out):
    steps = plan()
    mb_of = {s[1:4]: n for n, s in enumerate(s for s in steps if s[0] == "MS")}
    unit_of = {s[1:]: n for n, s in enumerate(s for s in steps if s[0] == "U")}
    unit_name = {n: u for u, n in unit_of.items()}
    last_kt = {"A": 1, "B": 1, "C": 3}
    pv_of = {s[1:5]: n for n, s in enumerate(s for s in steps if s[0] == "PV" and s[5] == last_kt[s[1]])}
    unit_pv = {n: pv_of[u[:4]] for u, n in unit_of.items()}
    f_of = {s[1:]: n for n, s in enumerate(s for s in steps if s[0] == "F")}
    xt_of = {s[1:]: n for n, s in enumerate(s for s in steps if s[0] == "XT")}

    with ExitStack() as stack:
        def sb(name, shape, dt=F32):
            return stack.enter_context(nc.sbuf_tensor(name, shape, dt))

        def ps(name, shape):
            return stack.enter_context(nc.psum_tensor(name, shape, F32))

        def sem(name):
            return stack.enter_context(nc.semaphore(name))

        ident = sb("ident", [P, P])
        ident_bf = sb("ident_bf", [P, P], BF16)
        mask_q = sb("mask_q", [P, P], BF16)
        mask_k = sb("mask_k", [P, P], BF16)
        expert_no = sb("expert_no", [P, E])
        half_neg = sb("half_neg", [P, QT])
        bias_sel = sb("bias_sel", [3 * E, E, P], BF16)
        first = [sb("first_0", [P, T + 2 * C + D + 5]), sb("first_1", [P, T])]
        rest = sb("rest", [P, N + 5 * C + 3 * C + E])
        ctx_room = sb("ctx_room", [P, B * TC + 2 * C])
        ctx_pack = ctx_room[0:CC, :]
        bias_row = sb("bias_row", [P, 6, C])
        w1T = sb("w1T", [P, E, 2 * HF])
        x0T = [first[0][:, 0:T], first[1][:, 0:T]]
        w_a = first[0][:, T:T + 2 * C + D]
        bias_col = first[0][:, T + 2 * C + D:]
        x_sb = rest[:, 0:N].rearrange("p (t c) -> p t c", c=C)
        wx = rest[:, N:N + 5 * C].rearrange("p (n c) -> p n c", c=C)
        w_oT = rest[:, N + 5 * C:N + 6 * C]
        w_ofT = rest[:, N + 6 * C:N + 8 * C].rearrange("p (i c) -> p i c", c=C)
        w_gT = rest[:, N + 8 * C:]
        ctxT, wc = ctx_pack[:, 0:B * TC], ctx_pack[:, B * TC:].rearrange("p (n c) -> p n c", c=C)
        xT = sb("xT", [P, N])
        x1T = x2T = xT
        q_stack = {p: sb(f"q_stack_{p}", [KROWS, H, N], BF16) for p in "AB"}
        q_stack["C"] = q_stack["A"]
        k_stack_a = sb("k_stack_a", [KROWS, N], BF16)
        k_stack_b = sb("k_stack_b", [KROWS, H, N], BF16)
        k_stack_c = sb("k_stack_c", [KROWS, H, B * TC], BF16)
        v_a = sb("v_a", [P, N // P, VW])
        v_b = sb("v_b", [P, N // P, H * VD + VW - VD])
        v_c = sb("v_c", [P, B * TC // P, H * VD + VW - VD])
        val_qk, val_qc = sb("val_qk", [P, 2, N]), sb("val_qc", [P, N])
        val_q, val_k = val_qk[:, 0, :], val_qk[:, 1, :]
        part_q = sb("part_q", [P, 3, N], BF16)
        part_qc = sb("part_qc", [P, 3, N], BF16)
        part_k = sb("part_k", [P, 3, N], BF16)
        b1_stack = sb("b1_stack", [3 * E, 2 * HF], BF16)
        NMB = len(mb_of)
        mneg = sb("mneg", [P, NMB, 3, 8])
        mpart = sb("mpart", [P, NMB, QT, 3, 8], BF16)
        mrow = sb("mrow", [24, NROW, T], BF16)
        probs = sb("probs", [P, NPT, 1024])
        y_sb = sb("y_sb", [P, 8, 512])
        val_c = y_sb[:, 2:4, :].rearrange("p a b -> p (a b)")
        part_c = y_sb[:, 4:7, :].bitcast(BF16)
        ysum = sb("ysum", [P, 32, 1])
        ytok = sb("ytok", [P, B + 1, QT * C])
        yT = first[1]
        xpb = sb("xpb", [P, N // P, C])
        z = ctx_room[:, 4 * HF:].rearrange("p (t c) -> p t c", c=C)
        stats = sb("stats", [P, QT, 6])
        mv = sb("mv", [P, QT, 2])
        rstd = sb("rstd", [P, 6, QT])
        x1 = sb("x1", [P, N // P, C])
        x2 = x1
        b1_sb = x1[0:E].rearrange("e t c -> e (t c)")
        b1_hi = sb("b1_hi", [E, 2 * HF], BF16)
        b1_low = y_sb[0:E, 7, :].bitcast(BF16).rearrange("e (r n) -> e r n", r=2)
        b1_part = [b1_hi[:], b1_low[:, 0, :], b1_low[:, 1, :]]
        warm = sb("warm", [P, 1])
        gate = sb("gate", [P, B, 11, QT, 8])
        gate_i = sb("gate_i", [P, B, QT, 8], U32)
        tanh_b = val_qk[:].rearrange("p a (b n) -> p (a b) n", n=HF)
        gated = val_qc[:].rearrange("p (a n) -> p a n", n=HF)
        gsum = ctx_room[:, 0:4 * HF].rearrange("p (b t n) -> p b t n", b=B, t=QT)
        gT = sb("gT", [P, 512])
        fin = x_sb

        region = {"w0": ps("w0", [P, 512]), "w1": ps("w1", [P, 512]), "t0": ps("t0", [P, 1024]),
                  "t1": ps("t1", [P, 1024]), "y": ps("y", [P, 512]), "m": ps("m", [P, 512])}
        full = {r: sem(f"full_{r}") for r in region}
        free = {r: sem(f"free_{r}") for r in region}

        ld_first, ld_second, ld_ctx, ld_rest, ld_row, ld_b1, ld_w1 = map(
            sem, ("ld_first", "ld_second", "ld_ctx", "ld_rest", "ld_row", "ld_b1", "ld_w1"))
        s_ident, s_ident_bf, s_mask, s_small, s_sel = map(
            sem, ("ident_made", "ident_bf_made", "masks_made", "small_made", "sel_made"))
        cleared = {k: sem(f"cleared_{k}") for k in (
            "qA0", "qA1", "qB", "qC0", "qC1", "kA", "kB", "kC", "vA", "vB", "vC")}
        chain_pool, chain_dve, chain_act = sem("chain_pool"), sem("chain_dve"), sem("chain_act")
        s_bias, s_warm = sem("bias_scaled"), sem("warm_made")
        s_parts = {k: sem(f"parts_{k}") for k in (
            "qA0", "qA1", "qB0", "kB0", "qC0", "qB1", "kB1", "qC1", "kC", "b1")}
        s_stack = {k: sem(f"stack_{k}") for k in (*s_parts, "kA0", "kA1")}
        s_mpart = sem("max_parts")
        s_shift = [sem(f"shift_{n}") for n in range(NMB)]
        s_pv = sem("pv_done")
        s_ytok, s_xres, s_var, s_rstd, s_xn = map(sem, ("y_normed", "residual_ready", "variance", "rstd", "x_normed"))
        s_lmax, s_gexp, s_comb, s_tanh, s_gated, s_fin, s_store = map(
            sem, ("gate_max", "gate_exp", "gate_comb", "tanh_done", "gated_sum", "fin_ready", "stored"))

        block = stack.enter_context(nc.Block())
        filled = {}
        fills = {r: 0 for r in region}

        def wait_full(eng, name):
            r, k = filled[name]
            eng.wait_ge(full[r], k + 1)
            return region[r]

        def emptied(ins, name):
            ins.then_inc(free[filled[name][0]], 1)

        def wait_emptied(eng, name):
            r, k = filled[name]
            eng.wait_ge(free[r], k + 1)

        def y_slot(part, b, g):
            return y_sb[:, {"A": 2 * b, "B": 4 - 4 * b, "C": 6 - 4 * b}[part] + g, :]

        def words(t):
            return t.bitcast(F32)

        def head_values(v):
            return v[:, 0:H * VD].rearrange("p (h w) -> p h w", w=VD)[:, :, 0:D]

        def stack_key(part, b):
            return "kC" if part == "C" else f"k{part}{b}"

        def make_stack(eng, dst, parts, side, key):
            for part in range(3):
                eng.wait_ge(s_parts[key], part + 1)
                for term in TERMS:
                    if term[1 + side] == part:
                        eng.dma_start(dst(slice(term[0], term[0] + D)), parts[:, part, :]).then_inc(s_stack[key], 16)

        @block.tensor
        def _(pe):
            def take(r, name):
                if fills[r]:
                    pe.wait_ge(free[r], fills[r])
                filled[name] = (r, fills[r])
                fills[r] += 1
                return region[r]

            def give(ins, name):
                ins.then_inc(full[filled[name][0]], 1)

            turn = {"w": 0, "t": 0}

            def ring(kind, name):
                r = f"{kind}{turn[kind] % 2}"
                turn[kind] += 1
                return take(r, name)

            for b in range(B):
                if b == 0:
                    pe.wait_ge(ld_first, 16)
                else:
                    pe.wait_ge(ld_second, 16)
                o = ring("w", ("qkA", b))
                nc.tensor.matmul(o[:, 0:T], w_a[:, 0:C], x0T[b], start=True, stop=True)
                last = nc.tensor.matmul(o[:, T:2 * T], w_a[:, C:2 * C], x0T[b], start=True, stop=True)
                give(last, ("qkA", b))
            o = take("m", "vA")
            for i in range(N // P):
                last = nc.tensor.matmul(o[:, i * D:(i + 1) * D], x0T[i // QT][:, i % QT * P:(i % QT + 1) * P],
                                        w_a[:, 2 * C:2 * C + D], start=True, stop=True)
            give(last, "vA")
            pe.wait_ge(ld_ctx, 16)
            o = ring("t", "kC")
            for i in range(2):
                last = nc.tensor.matmul(o[:, i * 512:(i + 1) * 512], wc[:, 0, :],
                                        ctxT[:, i * 512:(i + 1) * 512], start=True, stop=True)
            give(last, "kC")

            for s in steps:
                kind = s[0]
                if kind == "S":
                    _, part, b, g, h, qt = s
                    head = 8 * g + h
                    if h == 0 and not qt and g == 0:
                        pe.wait_ge(s_stack[f"q{part}{b}"], STACKED)
                        pe.wait_ge(s_stack[stack_key(part, b)], 3 if part == "A" else STACKED)
                        pe.wait_ge(cleared["kA"], 1)
                        pe.wait_ge(s_ident_bf, 1)
                        pe.wait_ge(s_mask, 1)
                    o = ring("w", s)
                    q = q_stack[part]
                    q0 = b * T
                    if part == "A":
                        for i in range(QT):
                            last = nc.tensor.matmul(o[:, i * T:(i + 1) * T], q[:, head, q0 + i * P:q0 + (i + 1) * P],
                                                    k_stack_a[:, q0:q0 + T], start=True, stop=True)
                    elif part == "B":
                        nc.tensor.matmul(o[:, 0:P], q[:, head, q0:q0 + P], k_stack_b[:, head, q0:q0 + P],
                                         start=True, stop=False)
                        nc.tensor.matmul(o[:, 0:P], ident_bf[:], mask_q[:], start=False, stop=True)
                        nc.tensor.matmul(o[:, P:3 * P], q[:, head, q0 + P:q0 + T], k_stack_b[:, head, q0:q0 + T],
                                         start=True, stop=False)
                        last = nc.tensor.matmul(o[:, 2 * P:3 * P], ident_bf[:], mask_q[:], start=False, stop=True)
                    else:
                        last = nc.tensor.matmul(o[:], q[:, head, q0 + qt * P:q0 + (qt + 1) * P],
                                                k_stack_c[:, head, b * TC:(b + 1) * TC], start=True, stop=True)
                    give(last, s)
                elif kind == "VC":
                    o = ring("t", s)
                    for i in range(4):
                        c0 = (4 * s[1] + i) * P
                        last = nc.tensor.matmul(o[:, i * P:(i + 1) * P], ctxT[:, c0:c0 + P], wc[:, 1, :],
                                                start=True, stop=True)
                    give(last, s)
                elif kind == "MT":
                    mb = mb_of[s[1:4]]
                    pe.wait_ge(s_mpart, mb + 1)
                    o = take("m", s).bitcast(BF16)
                    for i in range(QT):
                        last = nc.tensor.transpose(o[0:24, i * P:(i + 1) * P],
                                                   mpart[:, mb, i, :, :].rearrange("p r h -> p (r h)"), ident_bf[:])
                    give(last, s)
                elif kind == "U":
                    _, part, b, g, hh, j = s
                    pe.wait_ge(s_shift[mb_of[(part, b, g)]], 16)
                    o = ring("t", s)
                    q = q_stack[part]
                    q0 = b * T
                    if part == "A":
                        for kt in range(2):
                            rhs = q[:, 8 * g + j:8 * g + j + 5:4, q0:q0 + T]
                            last = nc.tensor.matmul(o[:, kt * 512:(kt + 1) * 512],
                                                    k_stack_a[:, q0 + kt * P:q0 + (kt + 1) * P], rhs,
                                                    start=True, stop=True)
                    elif part == "B":
                        for i in range(2):
                            head = 8 * g + 4 * hh + j + i
                            c0 = i * 512
                            nc.tensor.matmul(o[:, c0:c0 + T], k_stack_b[:, head, q0:q0 + P], q[:, head, q0:q0 + T],
                                             start=True, stop=False)
                            nc.tensor.matmul(o[:, c0:c0 + P], ident_bf[:], mask_k[:], start=False, stop=True)
                            nc.tensor.matmul(o[:, c0 + T:c0 + T + P], k_stack_b[:, head, q0 + P:q0 + T],
                                             q[:, head, q0 + P:q0 + T], start=True, stop=False)
                            last = nc.tensor.matmul(o[:, c0 + T:c0 + T + P], ident_bf[:], mask_k[:],
                                                    start=False, stop=True)
                    else:
                        head = 8 * g + 4 * hh + j
                        for kt in range(4):
                            k0 = b * TC + kt * P
                            last = nc.tensor.matmul(o[:, kt * T:(kt + 1) * T], k_stack_c[:, head, k0:k0 + P],
                                                    q[:, head, q0:q0 + T], start=True, stop=True)
                    give(last, s)
                elif kind == "PV":
                    _, part, b, g, hh, kt = s
                    if kt == 0:
                        units = [n for u, n in unit_of.items() if u[:4] == s[1:5]]
                        for n in sorted(units)[-2:]:
                            wait_emptied(pe, ("U",) + unit_name[n])
                        if hh == 0:
                            y_open = take("y", ("Y", part, b, g))
                            value_key = {"A": "vA", "B": ("qcv", b), "C": ("VC", 1)}[part]
                            wait_emptied(pe, value_key)
                    for j in range(4):
                        head = 8 * g + 4 * hh + j
                        v_cols = slice(VD * head, VD * head + VW)
                        if part == "A":
                            u = unit_of[("A", b, g, 0, j)] % NPT
                            cols = slice(0, 2 * T)
                            v, p = v_a[:, 2 * b + kt, :], probs[:, u, kt * 512:(kt + 1) * 512]
                        elif part == "B":
                            u = unit_of[("B", b, g, hh, j // 2 * 2)] % NPT
                            cols = slice(hh * T + kt * P, (hh + 1) * T)
                            c0 = (j % 2) * 512 + kt * T
                            v, p = v_b[:, 2 * b + kt, v_cols], probs[:, u, c0:c0 + T - kt * P]
                        else:
                            u = unit_of[("C", b, g, hh, j)] % NPT
                            cols = slice(hh * T, (hh + 1) * T)
                            v, p = v_c[:, 4 * b + kt, v_cols], probs[:, u, kt * T:(kt + 1) * T]
                        last = nc.tensor.matmul(y_open[32 * j:32 * j + VW, cols], v, p, start=(kt == 0),
                                                stop=(kt == last_kt[part]), tile_position=(0, 32 * j))
                    if kt == last_kt[part]:
                        last.then_inc(s_pv, 1)
                elif kind == "TY":
                    _, part, b = s
                    o = ring("t", s)
                    pe.wait_ge(s_ident, 1)
                    wait_emptied(pe, ("Y", part, b, 1))
                    for qt in range(QT):
                        for g in range(2):
                            for hh in range(2):
                                c0 = qt * 512 + (2 * g + hh) * P
                                last = nc.tensor.transpose(o[:, c0:c0 + P],
                                                           y_slot(part, b, g)[:, hh * T + qt * P:hh * T + (qt + 1) * P],
                                                           ident[:])
                    give(last, s)
                elif kind == "YT":
                    if s[2]:
                        pe.wait_ge(s_ytok, s[1] + 1)
                    else:
                        wait_emptied(pe, ("TY", "A", s[1]))
                    o = take("m", s)
                    for i in range(QT):
                        last = nc.tensor.transpose(o[:, i * P:(i + 1) * P], ytok[:, s[1], i * C:(i + 1) * C], ident[:])
                    give(last, s)
                elif kind == "WO":
                    _, b, cross = s
                    wait_emptied(pe, ("YT", b, cross))
                    pe.wait_ge(ld_rest, 16)
                    o = take("m", s)
                    for i in range(QT):
                        last = nc.tensor.matmul(o[:, i * C:(i + 1) * C], yT[:, i * P:(i + 1) * P],
                                                wx[:, 4, :] if cross else w_oT, start=True, stop=True)
                    give(last, s)
                elif kind == "XT":
                    _, b, cross = s
                    pe.wait_ge(s_xn, xt_of[(b, cross)] + 1)
                    o = take("m", s)
                    src = x2 if cross else x1
                    for i in range(QT):
                        last = nc.tensor.transpose(o[:, i * P:(i + 1) * P], src[:, 2 * b + i, :], ident[:])
                    give(last, s)
                elif kind == "PROJ":
                    b = s[1]
                    wait_emptied(pe, ("XT", b, 0))
                    cols = slice(b * T, (b + 1) * T)
                    o = ring("w", ("qk", b))
                    nc.tensor.matmul(o[:, 0:T], wx[:, 0, :], x1T[:, cols], start=True, stop=True)
                    give(nc.tensor.matmul(o[:, T:2 * T], wx[:, 1, :], x1T[:, cols], start=True, stop=True), ("qk", b))
                    o = ring("w", ("qcv", b))
                    nc.tensor.matmul(o[:, 0:T], wx[:, 2, :], x1T[:, cols], start=True, stop=True)
                    for i in range(QT):
                        last = nc.tensor.matmul(o[:, T + i * C:T + (i + 1) * C],
                                                x1T[:, b * T + i * P:b * T + (i + 1) * P], wx[:, 3, :],
                                                start=True, stop=True)
                    give(last, ("qcv", b))
                elif kind == "GATE":
                    b = s[1]
                    wait_emptied(pe, ("XT", b, 1))
                    o = take("m", s)
                    for i in range(QT):
                        last = nc.tensor.matmul(o[:, i * E:(i + 1) * E], x2T[:, b * T + i * P:b * T + (i + 1) * P],
                                                w_gT, start=True, stop=True)
                    give(last, s)
                elif kind == "F":
                    _, b, e, t = s
                    if f_of[s[1:]] == 0:
                        pe.wait_ge(ld_w1, 16)
                        pe.wait_ge(s_stack["b1"], 48)
                        pe.wait_ge(s_sel, 1)
                    o = ring("w", s)
                    nc.tensor.matmul(o[:], x2T[:, b * T + t * P:b * T + (t + 1) * P], w1T[:, e, :], start=True, stop=False)
                    last = nc.tensor.matmul(o[:], bias_sel[:, e, :], b1_stack[:], start=False, stop=True)
                    give(last, s)
                elif kind == "OUT":
                    b = s[1]
                    pe.wait_ge(s_gated, f_of[(b, E - 1, QT - 1)] + 1)
                    o = take("m", ("gT", b))
                    for i in range(QT):
                        for c in range(2):
                            last = nc.tensor.transpose(o[:, c * T + i * P:c * T + (i + 1) * P],
                                                       gsum[:, b, i, c * P:(c + 1) * P], ident[:])
                    give(last, ("gT", b))
                    wait_emptied(pe, ("gT", b))
                    o = take("m", s)
                    for i in range(QT):
                        for c in range(2):
                            last = nc.tensor.matmul(o[:, i * C:(i + 1) * C], gT[:, c * T + i * P:c * T + (i + 1) * P],
                                                    w_ofT[:, c, :], start=(c == 0), stop=(c == 1))
                    give(last, s)

        @block.vector
        def _(dve):
            V = nc.vector
            linked = [0]

            def link(ins):
                linked[0] += 1
                ins.then_inc(chain_dve, 1)
                dve.wait_ge(chain_dve, linked[0])

            def split(val, part, done):
                link(V.tensor_tensor(val, val, part(0), ALU.subtract))
                V.tensor_copy(part(1), val).then_inc(done, 1)
                dve.wait_ge(done, 2)
                V.tensor_tensor(part(2), val, part(1), ALU.subtract).then_inc(done, 1)

            def variance(zt):
                V.bn_stats(stats[:, 0, :], zt[:, 0, :])
                link(V.bn_stats(stats[:, 1, :], zt[:, 1, :]))
                V.bn_aggr(mv[:, 0, :], stats[:, 0, :])
                V.bn_aggr(mv[:, 1, :], stats[:, 1, :]).then_inc(s_var, 1)

            def norm(zt, n, dst):
                dve.wait_ge(s_rstd, n + 1)
                for i in range(QT):
                    ins = V.tensor_scalar(dst[:, i, :], zt[:, i, :], mv[:, i, 0:1], rstd[:, n, i:i + 1],
                                          ALU.subtract, ALU.mult)
                return ins

            V.memset(warm[:], 0.0).then_inc(s_warm, 1)
            V.memset(words(q_stack["A"][:, :, 0:T]), 0.0).then_inc(cleared["qA0"], 1)
            V.memset(words(k_stack_a[MROW:MROW + 32, :]), ONES).then_inc(cleared["kA"], 1)
            dve.wait_ge(ld_first, 16)
            V.tensor_scalar(bias_col[:, 0:3], bias_col[:, 0:3], SCALE, None, ALU.mult).then_inc(s_bias, 1)
            for b in range(B):
                cols = slice(b * T, (b + 1) * T)
                wait_emptied(dve, ("qkA", b))
                split(val_q[:, cols], lambda r: part_q[:, r, cols], s_parts[f"qA{b}"])
                link(V.tensor_tensor(val_k[:, cols], val_k[:, cols], part_k[:, 0, cols], ALU.subtract))
                V.tensor_copy(k_stack_a[32:64, cols], val_k[32:64, cols]).then_inc(s_stack[f"kA{b}"], 1)
                link(V.tensor_copy(part_k[:, 1, cols], val_k[:, cols]))
                V.tensor_tensor(k_stack_a[96:128, cols], val_k[96:128, cols], part_k[96:128, 1, cols],
                                ALU.subtract).then_inc(s_stack[f"kA{b}"], 1)
            dve.wait_ge(ld_row, 16)
            dve.wait_ge(cleared["vA"], 1)
            o = wait_full(dve, "vA")
            ins = V.tensor_tensor(v_a[:, :, 0:D], o[:, 0:4 * D].rearrange("p (i d) -> p i d", d=D),
                                  bias_row[:, 0:1, 0:D].to_broadcast([P, 4, D]), ALU.add)
            emptied(ins, "vA")

            n_norm = 0
            for s in steps:
                kind = s[0]
                if kind == "S":
                    _, part, b, g, h, qt = s
                    mb = mb_of[(part, b, g)]
                    o = wait_full(dve, s)
                    if part == "A":
                        dst, src = mneg[:, mb, 0:2, h], o[:].rearrange("p (a k) -> p a k", a=2)
                    elif part == "B":
                        dst, src = mneg[:, mb, :, h], o[:, 0:3 * P].rearrange("p (a k) -> p a k", a=3)
                    else:
                        dst, src = mneg[:, mb, qt, h:h + 1], o[:]
                    emptied(V.tensor_reduce(out=dst, in_=src, axis=AX.X, op=ALU.max, negate=True), s)
                    last_s = s
                elif kind == "MS":
                    mb = mb_of[s[1:4]]
                    wait_emptied(dve, last_s)
                    if s[1] == "B":
                        link(V.tensor_tensor(mneg[:, mb, 1, :], mneg[:, mb, 1, :], mneg[:, mb, 2, :], ALU.min))
                    link(V.tensor_copy(mpart[:, mb, :, 0, :], mneg[:, mb, 0:2, :]))
                    link(V.tensor_tensor(mneg[:, mb, 0:2, :], mneg[:, mb, 0:2, :], mpart[:, mb, :, 0, :], ALU.subtract))
                    link(V.tensor_copy(mpart[:, mb, :, 1, :], mneg[:, mb, 0:2, :]))
                    V.tensor_tensor(mpart[:, mb, :, 2, :], mneg[:, mb, 0:2, :], mpart[:, mb, :, 1, :],
                                    ALU.subtract).then_inc(s_mpart, 1)
                elif kind == "MT":
                    mb = mb_of[s[1:4]]
                    if mb >= NROW:
                        dve.wait_ge(s_shift[mb - NROW], 16)
                    o = wait_full(dve, s).bitcast(BF16)
                    emptied(V.tensor_copy(mrow[:, mb % NROW, :], o[0:24, 0:T]), s)
                elif kind == "VC":
                    dve.wait_ge(cleared["vC"], 1)
                    o = wait_full(dve, s)
                    for i in range(4):
                        ins = V.tensor_tensor(head_values(v_c[:, 4 * s[1] + i, :]),
                                              o[:, i * P:(i + 1) * P].rearrange("p (h d) -> p h d", d=D),
                                              bias_row[:, 2, :].rearrange("p (h d) -> p h d", d=D), ALU.add)
                    emptied(ins, s)
                elif kind == "TY":
                    _, part, b = s
                    o = wait_full(dve, s).rearrange("p (n w) -> p n w", w=VW)
                    link(V.reciprocal(ysum[:], o[:, :, D:D + 1]))
                    dst = ytok[:, B if part == "C" else b, :].rearrange("p (n d) -> p n d", d=D)
                    emptied(V.tensor_tensor(dst, o[:, :, 0:D], ysum[:].to_broadcast([P, 32, D]), ALU.mult), s)
                    wait_emptied(dve, s)
                    if part == "C":
                        V.tensor_tensor(ytok[:, b, :], ytok[:, b, :], ytok[:, B, :], ALU.add).then_inc(s_ytok, 1)
                elif kind == "YT":
                    o = wait_full(dve, s)
                    emptied(V.tensor_copy(yT[:], o[:, 0:T]), s)
                elif kind == "WO":
                    _, b, cross = s
                    dve.wait_ge(s_xres, 1 if not cross else 2 + b)
                    o = wait_full(dve, s)
                    ins = V.tensor_tensor(z, o[:, 0:T].rearrange("p (i c) -> p i c", c=C),
                                          xpb[:, 2 * b:2 * b + 2, :], ALU.add)
                    emptied(ins, s)
                    wait_emptied(dve, s)
                    variance(z)
                elif kind == "LN":
                    _, b, cross = s
                    dve.wait_ge(s_parts["b1"], 3)
                    norm(z, n_norm, (x2 if cross else x1)[:, 2 * b:2 * b + 2, :]).then_inc(s_xn, 1)
                    n_norm += 1
                elif kind == "XT":
                    _, b, cross = s
                    o = wait_full(dve, s)
                    emptied(V.tensor_copy((x2T if cross else x1T)[:, b * T:(b + 1) * T], o[:, 0:T]), s)
                elif kind == "PROJ":
                    b = s[1]
                    cols = slice(b * T, (b + 1) * T)
                    wait_emptied(dve, ("qk", b))
                    split(val_q[:, cols], lambda r: part_q[:, r, cols], s_parts[f"qB{b}"])
                    o = wait_full(dve, ("qcv", b))
                    link(V.tensor_scalar(val_qc[:, cols], o[:, 0:T], SCALE, bias_col[:, 2:3], ALU.mult, ALU.add))
                    dve.wait_ge(cleared["vB"], 1)
                    for i in range(QT):
                        ins = V.tensor_tensor(head_values(v_b[:, 2 * b + i, :]),
                                              o[:, T + i * C:T + (i + 1) * C].rearrange("p (h d) -> p h d", d=D),
                                              bias_row[:, 1, :].rearrange("p (h d) -> p h d", d=D), ALU.add)
                    emptied(ins, ("qcv", b))
                    V.tensor_copy(part_qc[:, 0, cols], val_qc[:, cols]).then_inc(s_parts[f"qC{b}"], 1)
                    dve.wait_ge(s_parts[f"qC{b}"], 1)
                    split(val_qc[:, cols], lambda r: part_qc[:, r, cols], s_parts[f"qC{b}"])
                elif kind == "GATE":
                    b = s[1]
                    t = {k: gate[:, b, n, :, :] for n, k in enumerate(
                        ("logit", "stat", "small", "exp", "score", "top", "index", "weight", "one0", "one1", "comb"))}
                    small = lambda n: t["small"][:, :, n:n + 1]
                    o = wait_full(dve, s)
                    emptied(V.tensor_copy(t["logit"], o[:, 0:QT * E].rearrange("p (i e) -> p i e", e=E)), s)
                    wait_emptied(dve, s)
                    V.tensor_reduce(out=t["stat"][:, :, 0], in_=t["logit"], axis=AX.X, op=ALU.max,
                                    negate=True).then_inc(s_lmax, 1)
                    dve.wait_ge(s_gexp, b + 1)
                    link(V.reciprocal(small(0), t["stat"][:, :, 1:2]))
                    link(V.tensor_tensor(t["score"], t["exp"], small(0).to_broadcast([P, QT, E]), ALU.mult))
                    for i in range(QT):
                        link(V.max(out=t["top"][:, i, :], in_=t["score"][:, i, :]))
                        link(V.max_index(gate_i[:, b, i, :], t["top"][:, i, :], t["score"][:, i, :]))
                    link(V.tensor_copy(t["index"], gate_i[:, b]))
                    link(V.tensor_tensor(small(1), t["top"][:, :, 0:1], t["top"][:, :, 1:2], ALU.add))
                    link(V.tensor_scalar(small(2), small(1), EPS_TOP, None, ALU.add))
                    link(V.reciprocal(small(3), small(2)))
                    link(V.tensor_tensor(t["weight"][:, :, 0:2], t["top"][:, :, 0:2],
                                         small(3).to_broadcast([P, QT, 2]), ALU.mult))
                    link(V.tensor_tensor(small(4), t["weight"][:, :, 0:1], t["weight"][:, :, 1:2], ALU.add))
                    link(V.tensor_scalar(t["weight"][:, :, 2:4], t["weight"][:, :, 0:2], 0.5, None, ALU.mult))
                    for i in range(QT):
                        for k in range(2):
                            link(V.tensor_scalar(t[f"one{k}"][:, i, :], expert_no[:], t["index"][:, i, k:k + 1],
                                                 t["weight"][:, i, 2 + k:3 + k], ALU.is_equal, ALU.mult))
                    link(V.tensor_tensor(t["comb"], t["one0"], t["one1"], ALU.add))
                    for i in range(QT):
                        link(V.scalar_tensor_tensor(out=xpb[:, 2 * b + i, :], in0=bias_row[:, 5, :],
                                                    scalar=t["small"][:, i, 4:5], in1=x2[:, 2 * b + i, :],
                                                    op0=ALU.mult, op1=ALU.add))
                elif kind == "F":
                    _, b, e, t = s
                    n = f_of[s[1:]]
                    dve.wait_ge(s_tanh, n + 1)
                    o = wait_full(dve, s)
                    product = gated[:, n % 2, :]
                    emptied(V.scalar_tensor_tensor(out=product, in0=tanh_b[:, n % 4, :], scalar=1.0, in1=o[:, 0:HF],
                                                   op0=ALU.add, op1=ALU.mult), s)
                    wait_emptied(dve, s)
                    dst = gsum[:, b, t, :]
                    weight = gate[:, b, 10, t, e:e + 1]
                    if e == 0:
                        ins = V.tensor_scalar(dst, product, weight, None, ALU.mult)
                    else:
                        dve.wait_ge(s_gated, n - 1)
                        ins = V.scalar_tensor_tensor(out=dst, in0=product, scalar=weight, in1=dst,
                                                     op0=ALU.mult, op1=ALU.add)
                    ins.then_inc(s_gated, 1)
                elif kind == "OUT":
                    b = s[1]
                    o = wait_full(dve, ("gT", b))
                    emptied(V.tensor_copy(gT[:], o[:]), ("gT", b))
                    o = wait_full(dve, s)
                    ins = V.tensor_tensor(z, o[:, 0:T].rearrange("p (i c) -> p i c", c=C),
                                          xpb[:, 2 * b:2 * b + 2, :], ALU.add)
                    emptied(ins, s)
                    wait_emptied(dve, s)
                    variance(z)
                    norm(z, n_norm, fin[:, 2 * b:2 * b + 2, :]).then_inc(s_fin, 1)
                    n_norm += 1

        @block.scalar
        def _(act):
            A = nc.scalar
            act.wait_ge(s_warm, 1)
            A.activation(warm[:], warm[:], ACT.Exp)
            act.wait_ge(s_bias, 1)
            for b in range(B):
                cols = slice(b * T, (b + 1) * T)
                o = wait_full(act, ("qkA", b))
                A.activation(part_q[:, 0, cols], o[:, 0:T], ACT.Identity, bias=bias_col[:, 0:1],
                             scale=SCALE).then_inc(s_parts[f"qA{b}"], 1)
                A.activation(val_q[:, cols], o[:, 0:T], ACT.Identity, bias=bias_col[:, 0:1], scale=SCALE)
                A.activation(k_stack_a[0:32, cols], o[0:32, T:2 * T], ACT.Copy).then_inc(s_stack[f"kA{b}"], 1)
                A.activation(part_k[:, 0, cols], o[:, T:2 * T], ACT.Copy)
                emptied(A.activation(val_k[:, cols], o[:, T:2 * T], ACT.Copy), ("qkA", b))
            o = wait_full(act, "kC")
            A.activation(part_c[:, 0, :], o[:], ACT.Identity, bias=bias_col[:, 4:5]).then_inc(s_parts["kC"], 1)
            emptied(A.activation(val_c, o[:], ACT.Identity, bias=bias_col[:, 4:5]), "kC")

            for s in steps:
                kind = s[0]
                if kind == "U":
                    n = unit_of[s[1:]]
                    if n >= NPT:
                        act.wait_ge(s_pv, unit_pv[n - NPT] + 1)
                    o = wait_full(act, s)
                    dst = probs[:, n % NPT, :]
                    if s[1] == "B":
                        ins = A.activation(dst.rearrange("p (i c) -> p i c", i=2)[:, :, 0:T + P],
                                           o[:].rearrange("p (i c) -> p i c", i=2)[:, :, 0:T + P], ACT.Exp)
                    else:
                        ins = A.activation(dst, o[:], ACT.Exp)
                    emptied(ins, s)
                elif kind == "PV" and s[4:] == (0 if s[1] == "A" else 1, last_kt[s[1]]):
                    part, b, g, hh = s[1:5]
                    if (part, b, g) == ("A", 1, 0):
                        act.wait_ge(s_stack["kC"], STACKED)
                    if (part, b, g) == ("C", 0, 1):
                        act.wait_ge(s_stack["b1"], 48)
                    act.wait_ge(s_pv, pv_of[s[1:5]] + 1)
                    emptied(A.activation(y_slot(part, b, g), region["y"][:], ACT.Copy), ("Y", part, b, g))
                elif kind == "PROJ":
                    b = s[1]
                    cols = slice(b * T, (b + 1) * T)
                    name = ("qk", b)
                    o = wait_full(act, name)
                    act.wait_ge(s_stack[f"qA{b}"], STACKED)
                    A.activation(part_q[:, 0, cols], o[:, 0:T], ACT.Identity, bias=bias_col[:, 1:2],
                                 scale=SCALE).then_inc(s_parts[f"qB{b}"], 1)
                    A.activation(val_q[:, cols], o[:, 0:T], ACT.Identity, bias=bias_col[:, 1:2], scale=SCALE)
                    act.wait_ge(s_stack[f"kA{b}"], 3)
                    A.activation(part_k[:, 0, cols], o[:, T:2 * T], ACT.Identity,
                                 bias=bias_col[:, 3:4]).then_inc(s_parts[f"kB{b}"], 1)
                    emptied(A.activation(val_k[:, cols], o[:, T:2 * T], ACT.Identity, bias=bias_col[:, 3:4]), name)
                elif kind == "GATE":
                    b = s[1]
                    act.wait_ge(s_lmax, b + 1)
                    for i in range(QT):
                        ins = A.activation(gate[:, b, 3, i, :], gate[:, b, 0, i, :], ACT.Exp,
                                           bias=gate[:, b, 1, i, 0:1], accum_out=gate[:, b, 1, i, 1:2])
                    ins.then_inc(s_gexp, 1)
                elif kind == "F":
                    n = f_of[s[1:]]
                    if n >= 4:
                        act.wait_ge(s_gated, n - 3)
                    o = wait_full(act, s)
                    A.activation(tanh_b[:, n % 4, :], o[:, HF:2 * HF], ACT.Tanh, scale=0.5).then_inc(s_tanh, 1)

        @block.gpsimd
        def _(pool):
            G = nc.gpsimd
            linked = [0]

            def link(ins):
                linked[0] += 1
                ins.then_inc(chain_pool, 1)
                pool.wait_ge(chain_pool, linked[0])

            def split(val, part, done):
                link(G.tensor_tensor(val, val, part(0), ALU.subtract))
                G.tensor_copy(part(1), val).then_inc(done, 1)
                pool.wait_ge(done, 2)
                G.tensor_tensor(part(2), val, part(1), ALU.subtract).then_inc(done, 1)

            link(G.memset(ident[:], 0.0))
            G.affine_select(out=ident[:], in_=ident[:], compare_op=ALU.not_equal, fill=1.0, base=0,
                            pattern=[[-1, P]], channel_multiplier=1).then_inc(s_ident, 1)
            G.memset(words(q_stack["A"][:, :, T:N]), 0.0).then_inc(cleared["qA1"], 1)
            link(G.memset(ident_bf[:], 0.0))
            G.affine_select(out=ident_bf[:], in_=ident_bf[:], compare_op=ALU.not_equal, fill=1.0, base=0,
                            pattern=[[-1, P]], channel_multiplier=1).then_inc(s_ident_bf, 1)
            G.memset(mask_q[:], 0.0)
            link(G.memset(mask_k[:], 0.0))
            G.affine_select(out=mask_q[:], in_=mask_q[:], compare_op=ALU.is_ge, fill=NEG, base=0,
                            pattern=[[-1, P]], channel_multiplier=1)
            G.affine_select(out=mask_k[:], in_=mask_k[:], compare_op=ALU.is_ge, fill=NEG, base=0,
                            pattern=[[1, P]], channel_multiplier=-1).then_inc(s_mask, 1)
            G.memset(v_a[:], 1.0).then_inc(cleared["vA"], 1)
            G.memset(words(k_stack_c[:]), ONES).then_inc(cleared["kC"], 1)
            G.memset(v_c[:], 1.0).then_inc(cleared["vC"], 1)
            wait_emptied(pool, "kC")
            split(val_c, lambda r: part_c[:, r, :], s_parts["kC"])
            pool.wait_ge(cleared["kC"], 1)
            make_stack(pool, lambda r: k_stack_c[r, :, :], part_c, 1, "kC")
            pool.wait_ge(ld_row, 16)
            pool.wait_ge(ld_rest, 16)
            for i in range(N // P):
                ins = G.tensor_tensor(xpb[:, i, :], x_sb[:, i, :], bias_row[:, 3, :], ALU.add)
            ins.then_inc(s_xres, 1)
            G.memset(half_neg[:], -0.5)
            for e in range(E):
                ins = G.memset(expert_no[:, e:e + 1], float(e))
            ins.then_inc(s_small, 1)
            G.memset(words(q_stack["B"][:]), 0.0).then_inc(cleared["qB"], 1)
            G.memset(words(k_stack_b[:]), ONES).then_inc(cleared["kB"], 1)
            G.memset(v_b[:], 1.0).then_inc(cleared["vB"], 1)
            link(G.memset(bias_sel[:], 0.0))
            for r in range(3):
                ins = G.affine_select(out=bias_sel[:], in_=bias_sel[:], compare_op=ALU.not_equal, fill=1.0,
                                      base=-8 * r, pattern=[[-1, E], [0, P]], channel_multiplier=1)
                if r < 2:
                    link(ins)
            ins.then_inc(s_sel, 1)
            pool.wait_ge(ld_b1, 16)
            G.tensor_copy(b1_part[0], b1_sb).then_inc(s_parts["b1"], 1)
            pool.wait_ge(s_parts["b1"], 1)
            split(b1_sb, lambda r: b1_part[r], s_parts["b1"])
            pool.wait_ge(s_parts["b1"], 3)
            for r in range(3):
                pool.dma_start(b1_stack[E * r:E * r + E, :], b1_part[r]).then_inc(s_stack["b1"], 16)

            n_norm = 0
            for s in steps:
                kind = s[0]
                if kind in ("WO", "OUT"):
                    pool.wait_ge(s_var, n_norm + 1)
                    link(G.tensor_scalar(rstd[:, n_norm, :], mv[:, :, 1], EPS_LN, None, ALU.add))
                    G.tensor_tensor(rstd[:, n_norm, :], rstd[:, n_norm, :], half_neg[:], ALU.pow).then_inc(s_rstd, 1)
                    n_norm += 1
                elif kind == "XT" and not s[2]:
                    b = s[1]
                    pool.wait_ge(s_xn, xt_of[(b, 0)] + 1)
                    for i in range(QT):
                        ins = G.tensor_tensor(xpb[:, 2 * b + i, :], x1[:, 2 * b + i, :], bias_row[:, 4, :], ALU.add)
                    ins.then_inc(s_xres, 1)
                elif kind == "PROJ":
                    b = s[1]
                    cols = slice(b * T, (b + 1) * T)
                    wait_emptied(pool, ("qk", b))
                    split(val_k[:, cols], lambda r: part_k[:, r, cols], s_parts[f"kB{b}"])
                    pool.wait_ge(s_pv, pv_of[("A", b, 1, 0)] + 1)
                    pool.wait_ge(s_parts[f"kB{b}"], 3)
                    G.memset(words(q_stack["C"][2 * 32:3 * 32, :, cols]), 0.0).then_inc(cleared[f"qC{b}"], 1)
                    pool.wait_ge(cleared[f"qC{b}"], 1)
                    pool.wait_ge(cleared["kB"], 1)
                    make_stack(pool, lambda r: k_stack_b[r, :, cols], part_k[:, :, cols], 1, f"kB{b}")

        @block.sync
        def _(sp):
            sp.dma_start(first[0][:], packs["first_0"]).then_inc(ld_first, 16)
            sp.dma_start(first[1][:], packs["first_1"]).then_inc(ld_second, 16)
            sp.dma_start(ctx_pack, packs["ctx"]).then_inc(ld_ctx, 16)
            sp.dma_start(bias_row[:].rearrange("p n c -> p (n c)"), packs["rows"].partition_broadcast(P)).then_inc(ld_row, 16)

            for b in range(B):
                cols = slice(b * T, (b + 1) * T)
                sp.wait_ge(cleared[f"qA{b}"], 1)
                make_stack(sp, lambda r: q_stack["A"][r, :, cols], part_q[:, :, cols], 0, f"qA{b}")
            sp.dma_start(b1_sb, packs["b1"]).then_inc(ld_b1, 16)
            sp.dma_start(rest[:], packs["rest"]).then_inc(ld_rest, 16)
            sp.dma_start(w1T[:].rearrange("p e n -> p (e n)"), packs["w1T"]).then_inc(ld_w1, 16)

            for s in steps:
                kind = s[0]
                if kind == "MT":
                    _, part, b, g = s
                    mb = mb_of[s[1:4]]
                    wait_emptied(sp, s)
                    sp.dma_start(q_stack[part][MROW:MROW + 3, 8 * g:8 * g + 8, b * T:(b + 1) * T],
                                 mrow[:, mb % NROW, :]).then_inc(s_shift[mb], 16)
                elif kind == "PROJ":
                    b = s[1]
                    cols = slice(b * T, (b + 1) * T)
                    sp.wait_ge(cleared["qB"], 1)
                    make_stack(sp, lambda r: q_stack["B"][r, :, cols], part_q[:, :, cols], 0, f"qB{b}")
                    sp.wait_ge(cleared[f"qC{b}"], 1)
                    make_stack(sp, lambda r: q_stack["C"][r, :, cols], part_qc[:, :, cols], 0, f"qC{b}")
                elif kind == "OUT":
                    b = s[1]
                    sp.wait_ge(s_fin, b + 1)
                    sp.dma_start(out[b].rearrange("(t p) c -> p t c", p=P), fin[:, 2 * b:2 * b + 2, :]).then_inc(s_store, 16)
            sp.wait_ge(s_store, 16 * B)


def kernel(**inputs):
    import numpy as _np
    import concourse.bacc as _bacc
    from concourse import mybir as _mybir
    from concourse.bass_utils import run_bass_kernel_spmd as _run

    i = {k: _np.asarray(v) for k, v in inputs.items()}
    order = _np.arange(C).reshape(H, D).T.ravel()
    col = lambda k, o=slice(None): i[k][o].reshape(C, 1)
    xT = i["x"].transpose(2, 0, 1)
    bv = _np.zeros(C, i["L0_attn_bv"].dtype)
    bv[:D] = i["L0_attn_bv"]
    packs = {
        "first_0": [xT[:, 0], i["L0_attn_Wq"].T[:, order], _np.tile(i["L0_attn_Wk"].T, H), i["L0_attn_Wv"].T,
                    col("L0_attn_bq", order), col("L0_xattn_bq", order), col("L0_xattn_bcq", order),
                    col("L0_xattn_bk", order), col("L0_xattn_bck", order)],
        "first_1": [xT[:, 1]],
        "ctx": [i["ctx_512"].transpose(2, 0, 1).reshape(CC, B * TC), i["L0_xattn_Wck"][:, order], i["L0_xattn_Wcv"]],
        "rest": [i["x"].reshape(N // P, P, C).transpose(1, 0, 2).reshape(P, N),
                 i["L0_xattn_Wq"][:, order], i["L0_xattn_Wk"][:, order], i["L0_xattn_Wcq"][:, order],
                 i["L0_xattn_Wv"], i["L0_xattn_Wp"], i["L0_attn_Wo"].T,
                 i["L0_ffn_Wo"].T[:P], i["L0_ffn_Wo"].T[P:], i["L0_ffn_Wg"].T],
        "w1T": [i["L0_ffn_W1"].transpose(2, 0, 1).reshape(P, E * 2 * HF)],
        "b1": [i["L0_ffn_b1"]],
        "rows": [bv, i["L0_xattn_bv"], i["L0_xattn_bcv"], i["L0_attn_bo"], i["L0_xattn_bp"], i["L0_ffn_bo"]],
    }
    packs = {k: _np.ascontiguousarray(_np.concatenate(v, axis=-1)) for k, v in packs.items()}

    nc = _bacc.Bacc("TRN2", target_bir_lowering=False, num_devices=1)
    aps = {k: nc.dram_tensor(f"in_{k}", a.shape, _mybir.dt.from_np(a.dtype), kind="ExternalInput").ap()
           for k, a in packs.items()}
    out = nc.dram_tensor("out_0", (B, T, C), _mybir.dt.float32, kind="ExternalOutput").ap()
    build(nc, aps, out)
    r = _run(nc, [{f"in_{k}": a for k, a in packs.items()}], core_ids=[0])
    return r.results[0]["out_0"]
```

```python
from contextlib import ExitStack

import numpy as np

import concourse.bass as bass
from concourse import mybir

F32 = mybir.dt.float32
BF16 = mybir.dt.bfloat16
U32 = mybir.dt.uint32
ALU = mybir.AluOpType
ACT = mybir.ActivationFunctionType
AX = mybir.AxisListType

P = 128
B, T, C, H, D = 2, 256, 128, 16, 8
TC, CC = 512, 64
E, HF = 8, 256
N = B * T
QT = T // P
SCALE = float(D) ** -0.5
EPS_LN = 1e-5
EPS_TOP = 1e-9
NEG = -1.0e30
ONES = float(np.uint32(0x3F803F80).view(np.float32))
KROWS = 128
MROW = 64
VD = D + 1
VW = 32
TERMS = ((0, 0, 0), (8, 1, 0), (16, 2, 0), (32, 0, 1), (40, 1, 1), (96, 0, 2))
STACKED = 16 * len(TERMS)
NPT = 8
CROSS_ORDER = ("BC", "CB")
NROW = 4


COSTS = {"SA": (0.43, 0.62), "SB": (0.25, 0.5), "SC": (0.22, 0.62), "MS": (0.0, 0.95), "MT": (0.15, 0.33),
         "UA": (0.5, 0.93), "UB": (0.4, 0.72), "UC": (0.45, 0.93), "PA": (0.93, 0.5), "PB": (0.3, 0.5), "PC": (0.35, 0.5),
         "TY": (0.87, 0.9), "YT": (0.3, 0.5), "WO": (0.43, 1.1), "LN": (0.0, 0.6), "XT": (0.43, 0.5), "PROJ": (3.0, 3.0),
         "VC": (1.2, 0.85), "GATE": (0.3, 4.5), "F": (1.0, 0.85), "GT": (0.22, 0.5), "OUT": (0.43, 2.2)}
SHIFT, STACK = 3.8, 4.5
LEAD = 21.96
URGENCY = {"S": (1.12, 0.8), "U": (1.05, 0.61), "PV self": 0.6, "PV cross": 0.72, "F": 0.09, "VC": -0.21, "GT": -3.34, "OUT": -3.34}
FIRST_SELF = 1.0
FIRST_EXPERTS = 0.5


def plan():
    groups = [(p, b, g) for b in range(B) for p in "A" for g in range(2)]
    groups += [(p, b, g) for b in range(B) for p in CROSS_ORDER[b] for g in range(2)]
    scores, shifts, probs, values = [], [], [], []
    for p, b, g in groups:
        tiles = range(QT) if p == "C" else (None,)
        scores += [("S", p, b, g, h, qt) for h in range(8) for qt in tiles] + [("MS", p, b, g)]
        shifts += [("MT", p, b, g)]
        for hh in range(1 if p == "A" else 2):
            probs += [("U", p, b, g, hh, j) for j in range(0, 4, 2 if p == "B" else 1)]
            values += [("PV", p, b, g, hh, kt) for kt in range(4 if p == "C" else 2)]
    posts = [[("TY", "A", b), ("YT", b, 0), ("WO", b, 0), ("LN", b, 0), ("XT", b, 0), ("PROJ", b)] for b in range(B)]
    ends = [[("TY", p, b) for p in CROSS_ORDER[b]] + [("YT", b, 1), ("WO", b, 1), ("LN", b, 1), ("XT", b, 1), ("GATE", b)]
            + [("F", b, e, 0) for e in range(E)] + [("F", b, e, 1) for e in range(2)] + [("GT", b, 0), ("F", b, 2, 1), ("OUT", b, 0)]
            + [("F", b, e, 1) for e in range(3, E)] + [("GT", b, 1), ("OUT", b, 1)] for b in range(B)]
    streams = [posts[0], posts[1], ends[0], ends[1], shifts, probs, values, scores, [("VC", 0), ("VC", 1)]]
    last_kt = {"A": 1, "B": 1, "C": 3}
    opens = {("PV", p, b, g, 0, 0) for p, b, g in groups}
    closes = {("PV", p, b, g, 0 if p == "A" else 1, last_kt[p]) for p, b, g in groups}

    def needs(s):
        k = s[0]
        if k == "S" and s[1] != "A":
            return [(("PROJ", s[2]), STACK)]
        if k == "MT":
            return [(("MS",) + s[1:], 0.2)]
        if k == "U":
            n = probs.index(s) - NPT
            ring = [(("PV",) + probs[n][1:5] + (last_kt[probs[n][1]],), 0.0)] if n >= 0 else []
            return ring + [(("MT",) + s[1:4], SHIFT)]
        if s in (("PV", "C", 0, 0, 0, 0), ("F", 0, 0, 0)):
            extra = [(("VC", 1), 0.1)]
        else:
            extra = []
        if k == "PV":
            return extra + [(u, 0.1) for u in probs if u[:5] == ("U",) + s[1:5]]
        if k == "TY":
            part, b = s[1:]
            return [(("PV", part, b, 1, 0 if part == "A" else 1, last_kt[part]), 0.2)]
        return extra

    region = {"S": "w", "F": "w", "PROJ": "w", "U": "t", "TY": "t", "VC": "t", "MT": "m", "YT": "m", "WO": "m", "XT": "m",
              "GATE": "m", "GT": "m", "OUT": "m"}
    reader = {"U": "act", "PV": "act"}
    done, free_at, used = {}, {"pe": 0.0, "dve": 0.0, "act": 0.0}, {"w": [0.0, 0.0], "t": [0.0, 0.0], "m": [0.0], "y": [0.0]}
    last_of = [0.0] * len(streams)
    at, out = [0] * len(streams), []

    heads = {"SA": 1.0, "SB": 1.0, "SC": 0.5, "UA": 2.0, "UB": 2.0, "UC": 1.0}
    ahead = [0.0]

    def start(n, s):
        if s[0] == "S" and ahead[0] >= LEAD:
            return None
        if s[0] in ("YT", "OUT") and len({d for d in done if d[0] == "YT"}) > len({d for d in done if d[0] == "LN"}):
            return None
        need = needs(s)
        if any(d not in done for d, _ in need):
            return None
        t = max([free_at["pe"]] + [done[d] + lag for d, lag in need])
        if s[0] in ("YT", "WO", "XT", "PROJ", "GATE", "GT", "OUT") or s[0] == "F" and s[2:] == (0, 0):
            t = max(t, last_of[n])
        if s[0] == "GT":
            t += 0.3
        if s[0] == "LN":
            t = max(t, last_of[n] + 1.2)
        r = "y" if s in opens else "wt"[s[2] % 2] if s[0] == "F" else region.get(s[0])
        return max(t, used[r][0]) if r else t

    def urgency(s, t):
        if s[0] in ("U", "PV") and s[1:3] == ("A", 0):
            return FIRST_SELF
        if s[0] in ("S", "MS"):
            return URGENCY["S"][0 if free_at["dve"] - t < 0.8 else 1]
        if s[0] == "U":
            return URGENCY["U"][0 if free_at["act"] - t < 0.6 else 1]
        if s[0] == "PV":
            return URGENCY["PV self" if s[1] == "A" else "PV cross"]
        return URGENCY.get(s[0], 1.0) + (FIRST_EXPERTS if s[:2] == ("F", 0) else 0.0)

    while any(at[n] < len(q) for n, q in enumerate(streams)):
        best = None
        for n, q in enumerate(streams):
            if at[n] == len(q):
                continue
            t = start(n, q[at[n]])
            if t is None:
                continue
            rank = t - urgency(q[at[n]], t)
            if best is None or rank < best[0] - 0.01:
                best = (rank, t, n)
        _, t, n = best
        s = streams[n][at[n]]
        at[n] += 1
        if s[0] in "SU":
            ahead[0] += heads[s[0] + s[1]] * (1 if s[0] == "S" else -1)
        key = {"S": "S", "U": "U", "PV": "P"}.get(s[0])
        pe, rest = COSTS[key + s[1] if key else s[0]]
        if pe:
            free_at["pe"] = t + pe
        eng = reader.get(s[0], "dve")
        end = t + pe
        if s[0] != "PV" or s in closes:
            end = max(end, free_at[eng]) + rest
            free_at[eng] = end
        r = "y" if s in closes else "wt"[s[2] % 2] if s[0] == "F" else region.get(s[0])
        if r:
            used[r] = used[r][1:] + [end]
        done[s] = last_of[n] = end
        out.append(s)
    return out


def build(nc, packs, out):
    steps = plan()
    mb_of = {s[1:4]: n for n, s in enumerate(s for s in steps if s[0] == "MS")}
    unit_of = {s[1:]: n for n, s in enumerate(s for s in steps if s[0] == "U")}
    unit_name = {n: u for u, n in unit_of.items()}
    last_kt = {"A": 1, "B": 1, "C": 3}
    pv_of = {s[1:5]: n for n, s in enumerate(s for s in steps if s[0] == "PV" and s[5] == last_kt[s[1]])}
    unit_pv = {n: pv_of[u[:4]] for u, n in unit_of.items()}
    f_of = {s[1:]: n for n, s in enumerate(s for s in steps if s[0] == "F")}
    f_steps = [s for s in steps if s[0] == "F"]
    xt_of = {s[1:]: n for n, s in enumerate(s for s in steps if s[0] == "XT")}

    with ExitStack() as stack:
        def sb(name, shape, dt=F32):
            return stack.enter_context(nc.sbuf_tensor(name, shape, dt))

        def ps(name, shape):
            return stack.enter_context(nc.psum_tensor(name, shape, F32))

        def sem(name):
            return stack.enter_context(nc.semaphore(name))

        ident = sb("ident", [P, P])
        ident_bf = sb("ident_bf", [P, P], BF16)
        mask_q = sb("mask_q", [P, P], BF16)
        mask_k = sb("mask_k", [P, P], BF16)
        expert_no = sb("expert_no", [P, E])
        half_neg = sb("half_neg", [P, QT])
        bias_sel = sb("bias_sel", [3 * E, E, P], BF16)
        first = [sb("first_0", [P, T + 2 * C + D + 5]), sb("first_1", [P, T])]
        rest = sb("rest", [P, N + 5 * C + 3 * C + E])
        ctx_room = sb("ctx_room", [P, B * TC + 2 * C])
        ctx_pack = ctx_room[0:CC, :]
        bias_row = sb("bias_row", [P, 6, C])
        w1T = sb("w1T", [P, E, 2 * HF])
        x0T = [first[0][:, 0:T], first[1][:, 0:T]]
        w_a = first[0][:, T:T + 2 * C + D]
        bias_col = first[0][:, T + 2 * C + D:]
        x_sb = rest[:, 0:N].rearrange("p (t c) -> p t c", c=C)
        wx = rest[:, N:N + 5 * C].rearrange("p (n c) -> p n c", c=C)
        w_oT = rest[:, N + 5 * C:N + 6 * C]
        w_ofT = rest[:, N + 6 * C:N + 8 * C].rearrange("p (i c) -> p i c", c=C)
        w_gT = rest[:, N + 8 * C:]
        ctxT, wc = ctx_pack[:, 0:B * TC], ctx_pack[:, B * TC:].rearrange("p (n c) -> p n c", c=C)
        xT = sb("xT", [P, N])
        x1T = x2T = xT
        q_stack = {p: sb(f"q_stack_{p}", [KROWS, H, N], BF16) for p in "AB"}
        q_stack["C"] = q_stack["A"]
        k_stack_a = sb("k_stack_a", [KROWS, N], BF16)
        k_stack_b = sb("k_stack_b", [KROWS, H, N], BF16)
        k_stack_c = sb("k_stack_c", [KROWS, H, B * TC], BF16)
        v_a = sb("v_a", [P, N // P, VW])
        v_b = sb("v_b", [P, N // P, H * VD + VW - VD])
        v_c = sb("v_c", [P, B * TC // P, H * VD + VW - VD])
        val_qk, val_qc = sb("val_qk", [P, 2, N]), sb("val_qc", [P, N])
        val_q, val_k = val_qk[:, 0, :], val_qk[:, 1, :]
        part_q = sb("part_q", [P, 3, N], BF16)
        part_qc = sb("part_qc", [P, 3, N], BF16)
        part_k = sb("part_k", [P, 3, N], BF16)
        b1_stack = sb("b1_stack", [3 * E, 2 * HF], BF16)
        NMB = len(mb_of)
        mneg = sb("mneg", [P, NMB, 3, 8])
        mpart = sb("mpart", [P, NMB, QT, 3, 8], BF16)
        mrow = sb("mrow", [24, NROW, T], BF16)
        probs = sb("probs", [P, NPT, 1024])
        y_sb = sb("y_sb", [P, 8, 512])
        val_c = y_sb[:, 2:4, :].rearrange("p a b -> p (a b)")
        part_c = y_sb[:, 4:7, :].bitcast(BF16)
        ysum = sb("ysum", [P, 32, 1])
        ytok = sb("ytok", [P, B + 1, QT * C])
        yT = first[1]
        xpb = sb("xpb", [P, N // P, C])
        z = sb("z", [P, QT, C])
        stats = sb("stats", [P, QT, 6])
        mv = sb("mv", [P, QT, 2])
        rstd = sb("rstd", [P, 4 * B, QT])
        x1 = sb("x1", [P, N // P, C])
        x2 = x1
        b1_sb = x1[0:E].rearrange("e t c -> e (t c)")
        b1_hi = sb("b1_hi", [E, 2 * HF], BF16)
        b1_low = y_sb[0:E, 7, :].bitcast(BF16).rearrange("e (r n) -> e r n", r=2)
        b1_part = [b1_hi[:], b1_low[:, 0, :], b1_low[:, 1, :]]
        warm = sb("warm", [P, 1])
        gate = sb("gate", [P, B, 11, QT, 8])
        gate_i = sb("gate_i", [P, B, QT, 8], U32)
        tanh_b = val_qk[:].rearrange("p a (b n) -> p (a b) n", n=HF)
        gated = val_qc[:].rearrange("p (a n) -> p a n", n=HF)
        gsum = ctx_room[:, 0:4 * HF].rearrange("p (b t n) -> p b t n", b=B, t=QT)
        gT = [part_q[:, 0:2, :].bitcast(F32), part_k[:, 0:2, :].bitcast(F32)]
        fin = x_sb

        region = {"w0": ps("w0", [P, 512]), "w1": ps("w1", [P, 512]), "t0": ps("t0", [P, 1024]),
                  "t1": ps("t1", [P, 1024]), "y": ps("y", [P, 512]), "m": ps("m", [P, 512])}
        full = {r: sem(f"full_{r}") for r in region}
        free = {r: sem(f"free_{r}") for r in region}

        ld_first, ld_second, ld_ctx, ld_rest, ld_row, ld_b1, ld_w1 = map(
            sem, ("ld_first", "ld_second", "ld_ctx", "ld_rest", "ld_row", "ld_b1", "ld_w1"))
        s_ident, s_ident_bf, s_mask, s_small, s_sel = map(
            sem, ("ident_made", "ident_bf_made", "masks_made", "small_made", "sel_made"))
        cleared = {k: sem(f"cleared_{k}") for k in (
            "qA0", "qA1", "qB", "qC0", "qC1", "kA", "kB", "kC", "vA", "vB", "vC")}
        chain_pool, chain_dve = sem("chain_pool"), sem("chain_dve")
        s_bias, s_warm = sem("bias_scaled"), sem("warm_made")
        s_parts = {k: sem(f"parts_{k}") for k in (
            "qA0", "qA1", "qB0", "kB0", "qC0", "qB1", "kB1", "qC1", "kC", "b1")}
        s_stack = {k: sem(f"stack_{k}") for k in (*s_parts, "kA0", "kA1")}
        s_stack_low = [sem(f"stack_kB{b}_low") for b in range(B)]
        s_mpart = sem("max_parts")
        s_shift = [sem(f"shift_{n}") for n in range(NMB)]
        s_pv = sem("pv_done")
        s_ytok, s_xres, s_var, s_rstd, s_xn = map(sem, ("y_normed", "residual_ready", "variance", "rstd", "x_normed"))
        s_lmax, s_tanh, s_gated, s_fin, s_store = map(
            sem, ("gate_max", "tanh_done", "gated_sum", "fin_ready", "stored"))

        block = stack.enter_context(nc.Block())
        filled = {}
        fills = {r: 0 for r in region}

        def wait_full(eng, name):
            r, k = filled[name]
            eng.wait_ge(full[r], k + 1)
            return region[r]

        def emptied(ins, name):
            ins.then_inc(free[filled[name][0]], 1)

        def wait_emptied(eng, name):
            r, k = filled[name]
            eng.wait_ge(free[r], k + 1)

        def y_slot(part, b, g):
            return y_sb[:, {"A": 2 * b, "B": 4 - 4 * b, "C": 6 - 4 * b}[part] + g, :]

        def words(t):
            return t.bitcast(F32)

        def head_values(v):
            return v[:, 0:H * VD].rearrange("p (h w) -> p h w", w=VD)[:, :, 0:D]

        def stack_key(part, b):
            return "kC" if part == "C" else f"k{part}{b}"

        def make_stack(eng, dst, parts, side, key, which=range(3), done=None):
            for part in which:
                eng.wait_ge(s_parts[key], part + 1)
                for term in TERMS:
                    if term[1 + side] == part:
                        eng.dma_start(dst(slice(term[0], term[0] + D)), parts[:, part, :]).then_inc(done or s_stack[key], 16)

        @block.tensor
        def _(pe):
            def take(r, name):
                if fills[r]:
                    pe.wait_ge(free[r], fills[r])
                filled[name] = (r, fills[r])
                fills[r] += 1
                return region[r]

            def give(ins, name):
                ins.then_inc(full[filled[name][0]], 1)

            turn = {"w": 0, "t": 0}

            def ring(kind, name):
                r = f"{kind}{turn[kind] % 2}"
                turn[kind] += 1
                return take(r, name)

            for b in range(B):
                if b == 0:
                    pe.wait_ge(ld_first, 16)
                else:
                    pe.wait_ge(ld_second, 16)
                for i, name in enumerate(("qA", "kA")):
                    o = ring("w", (name, b))
                    give(nc.tensor.matmul(o[:, 0:T], w_a[:, i * C:(i + 1) * C], x0T[b], start=True, stop=True), (name, b))
            o = take("m", "vA")
            for i in range(N // P):
                last = nc.tensor.matmul(o[:, i * D:(i + 1) * D], x0T[i // QT][:, i % QT * P:(i % QT + 1) * P],
                                        w_a[:, 2 * C:2 * C + D], start=True, stop=True)
            give(last, "vA")
            pe.wait_ge(ld_ctx, 16)
            o = ring("t", "kC")
            for i in range(2):
                last = nc.tensor.matmul(o[:, i * 512:(i + 1) * 512], wc[:, 0, :],
                                        ctxT[:, i * 512:(i + 1) * 512], start=True, stop=True)
            give(last, "kC")

            for s in steps:
                kind = s[0]
                if kind == "S":
                    _, part, b, g, h, qt = s
                    head = 8 * g + h
                    if h == 0 and not qt and g == 0:
                        pe.wait_ge(s_stack[f"q{part}{b}"], STACKED)
                        pe.wait_ge(s_stack[stack_key(part, b)], {"A": 3, "B": STACKED // 2, "C": STACKED}[part])
                        if part == "B":
                            pe.wait_ge(s_stack_low[b], STACKED // 2)
                        pe.wait_ge(cleared["kA"], 1)
                        pe.wait_ge(s_ident_bf, 1)
                        pe.wait_ge(s_mask, 1)
                    o = ring("w", s)
                    q = q_stack[part]
                    q0 = b * T
                    if part == "A":
                        for i in range(QT):
                            last = nc.tensor.matmul(o[:, i * T:(i + 1) * T], q[:, head, q0 + i * P:q0 + (i + 1) * P],
                                                    k_stack_a[:, q0:q0 + T], start=True, stop=True)
                    elif part == "B":
                        nc.tensor.matmul(o[:, 0:P], q[:, head, q0:q0 + P], k_stack_b[:, head, q0:q0 + P],
                                         start=True, stop=False)
                        nc.tensor.matmul(o[:, 0:P], ident_bf[:], mask_q[:], start=False, stop=True)
                        nc.tensor.matmul(o[:, P:3 * P], q[:, head, q0 + P:q0 + T], k_stack_b[:, head, q0:q0 + T],
                                         start=True, stop=False)
                        last = nc.tensor.matmul(o[:, 2 * P:3 * P], ident_bf[:], mask_q[:], start=False, stop=True)
                    else:
                        last = nc.tensor.matmul(o[:], q[:, head, q0 + qt * P:q0 + (qt + 1) * P],
                                                k_stack_c[:, head, b * TC:(b + 1) * TC], start=True, stop=True)
                    give(last, s)
                elif kind == "VC":
                    o = ring("t", s)
                    for i in range(4):
                        c0 = (4 * s[1] + i) * P
                        last = nc.tensor.matmul(o[:, i * P:(i + 1) * P], ctxT[:, c0:c0 + P], wc[:, 1, :],
                                                start=True, stop=True)
                    give(last, s)
                elif kind == "MT":
                    mb = mb_of[s[1:4]]
                    pe.wait_ge(s_mpart, mb + 1)
                    o = take("m", s).bitcast(BF16)
                    for i in range(QT):
                        last = nc.tensor.transpose(o[0:24, i * P:(i + 1) * P],
                                                   mpart[:, mb, i, :, :].rearrange("p r h -> p (r h)"), ident_bf[:])
                    give(last, s)
                elif kind == "U":
                    _, part, b, g, hh, j = s
                    pe.wait_ge(s_shift[mb_of[(part, b, g)]], 16)
                    o = ring("t", s)
                    q = q_stack[part]
                    q0 = b * T
                    if part == "A":
                        for kt in range(2):
                            rhs = q[:, 8 * g + j:8 * g + j + 5:4, q0:q0 + T]
                            last = nc.tensor.matmul(o[:, kt * 512:(kt + 1) * 512],
                                                    k_stack_a[:, q0 + kt * P:q0 + (kt + 1) * P], rhs,
                                                    start=True, stop=True)
                    elif part == "B":
                        for i in range(2):
                            head = 8 * g + 4 * hh + j + i
                            c0 = i * 512
                            nc.tensor.matmul(o[:, c0:c0 + T], k_stack_b[:, head, q0:q0 + P], q[:, head, q0:q0 + T],
                                             start=True, stop=False)
                            nc.tensor.matmul(o[:, c0:c0 + P], ident_bf[:], mask_k[:], start=False, stop=True)
                            nc.tensor.matmul(o[:, c0 + T:c0 + T + P], k_stack_b[:, head, q0 + P:q0 + T],
                                             q[:, head, q0 + P:q0 + T], start=True, stop=False)
                            last = nc.tensor.matmul(o[:, c0 + T:c0 + T + P], ident_bf[:], mask_k[:],
                                                    start=False, stop=True)
                    else:
                        head = 8 * g + 4 * hh + j
                        for kt in range(4):
                            k0 = b * TC + kt * P
                            last = nc.tensor.matmul(o[:, kt * T:(kt + 1) * T], k_stack_c[:, head, k0:k0 + P],
                                                    q[:, head, q0:q0 + T], start=True, stop=True)
                    give(last, s)
                elif kind == "PV":
                    _, part, b, g, hh, kt = s
                    if kt == 0:
                        units = [n for u, n in unit_of.items() if u[:4] == s[1:5]]
                        for n in sorted(units)[-2:]:
                            wait_emptied(pe, ("U",) + unit_name[n])
                        if hh == 0:
                            y_open = take("y", ("Y", part, b, g))
                            value_key = {"A": "vA", "B": ("qcv", b), "C": ("VC", 1)}[part]
                            wait_emptied(pe, value_key)
                    for j in range(4):
                        head = 8 * g + 4 * hh + j
                        v_cols = slice(VD * head, VD * head + VW)
                        if part == "A":
                            u = unit_of[("A", b, g, 0, j)] % NPT
                            cols = slice(0, 2 * T)
                            v, p = v_a[:, 2 * b + kt, :], probs[:, u, kt * 512:(kt + 1) * 512]
                        elif part == "B":
                            u = unit_of[("B", b, g, hh, j // 2 * 2)] % NPT
                            cols = slice(hh * T + kt * P, (hh + 1) * T)
                            c0 = (j % 2) * 512 + kt * T
                            v, p = v_b[:, 2 * b + kt, v_cols], probs[:, u, c0:c0 + T - kt * P]
                        else:
                            u = unit_of[("C", b, g, hh, j)] % NPT
                            cols = slice(hh * T, (hh + 1) * T)
                            v, p = v_c[:, 4 * b + kt, v_cols], probs[:, u, kt * T:(kt + 1) * T]
                        last = nc.tensor.matmul(y_open[32 * j:32 * j + VW, cols], v, p, start=(kt == 0),
                                                stop=(kt == last_kt[part]), tile_position=(0, 32 * j))
                    if kt == last_kt[part]:
                        last.then_inc(s_pv, 1)
                elif kind == "TY":
                    _, part, b = s
                    o = ring("t", s)
                    pe.wait_ge(s_ident, 1)
                    wait_emptied(pe, ("Y", part, b, 1))
                    for qt in range(QT):
                        for g in range(2):
                            for hh in range(2):
                                c0 = qt * 512 + (2 * g + hh) * P
                                last = nc.tensor.transpose(o[:, c0:c0 + P],
                                                           y_slot(part, b, g)[:, hh * T + qt * P:hh * T + (qt + 1) * P],
                                                           ident[:])
                    give(last, s)
                elif kind == "YT":
                    if s[2]:
                        pe.wait_ge(s_ytok, s[1] + 1)
                    else:
                        wait_emptied(pe, ("TY", "A", s[1]))
                    o = take("m", s)
                    for i in range(QT):
                        last = nc.tensor.transpose(o[:, i * P:(i + 1) * P], ytok[:, s[1], i * C:(i + 1) * C], ident[:])
                    give(last, s)
                elif kind == "WO":
                    _, b, cross = s
                    wait_emptied(pe, ("YT", b, cross))
                    pe.wait_ge(ld_rest, 16)
                    o = take("m", s)
                    for i in range(QT):
                        last = nc.tensor.matmul(o[:, i * C:(i + 1) * C], yT[:, i * P:(i + 1) * P],
                                                wx[:, 4, :] if cross else w_oT, start=True, stop=True)
                    give(last, s)
                elif kind == "XT":
                    _, b, cross = s
                    pe.wait_ge(s_xn, xt_of[(b, cross)] + 1)
                    o = take("m", s)
                    src = x2 if cross else x1
                    for i in range(QT):
                        last = nc.tensor.transpose(o[:, i * P:(i + 1) * P], src[:, 2 * b + i, :], ident[:])
                    give(last, s)
                elif kind == "PROJ":
                    b = s[1]
                    wait_emptied(pe, ("XT", b, 0))
                    cols = slice(b * T, (b + 1) * T)
                    for i, name in enumerate("qk"):
                        o = ring("w", (name, b))
                        give(nc.tensor.matmul(o[:, 0:T], wx[:, i, :], x1T[:, cols], start=True, stop=True), (name, b))
                    o = ring("w", ("qcv", b))
                    nc.tensor.matmul(o[:, 0:T], wx[:, 2, :], x1T[:, cols], start=True, stop=True)
                    for i in range(QT):
                        last = nc.tensor.matmul(o[:, T + i * C:T + (i + 1) * C],
                                                x1T[:, b * T + i * P:b * T + (i + 1) * P], wx[:, 3, :],
                                                start=True, stop=True)
                    give(last, ("qcv", b))
                elif kind == "GATE":
                    b = s[1]
                    wait_emptied(pe, ("XT", b, 1))
                    o = take("m", s)
                    for i in range(QT):
                        last = nc.tensor.matmul(o[:, i * E:(i + 1) * E], x2T[:, b * T + i * P:b * T + (i + 1) * P],
                                                w_gT, start=True, stop=True)
                    give(last, s)
                elif kind == "F":
                    _, b, e, t = s
                    if f_of[s[1:]] == 0:
                        pe.wait_ge(ld_w1, 16)
                        pe.wait_ge(s_stack["b1"], 48)
                        pe.wait_ge(s_sel, 1)
                    o = ring("wt"[e % 2], s)[:, 0:2 * HF]
                    nc.tensor.matmul(o, x2T[:, b * T + t * P:b * T + (t + 1) * P], w1T[:, e, :], start=True, stop=False)
                    last = nc.tensor.matmul(o, bias_sel[:, e, :], b1_stack[:], start=False, stop=True)
                    give(last, s)
                elif kind == "GT":
                    _, b, t = s
                    pe.wait_ge(s_gated, f_of[(b, E - 1, t)] + 1)
                    o = take("m", s)
                    for c in range(2):
                        last = nc.tensor.transpose(o[:, c * P:(c + 1) * P], gsum[:, b, t, c * P:(c + 1) * P], ident[:])
                    give(last, s)
                elif kind == "OUT":
                    _, b, t = s
                    wait_emptied(pe, ("GT", b, t))
                    o = take("m", s)
                    for c in range(2):
                        last = nc.tensor.matmul(o[:, 0:C], gT[b][:, t, c * P:(c + 1) * P], w_ofT[:, c, :],
                                                start=(c == 0), stop=(c == 1))
                    give(last, s)

        @block.vector
        def _(dve):
            V = nc.vector
            linked = [0]

            def link(ins):
                linked[0] += 1
                ins.then_inc(chain_dve, 1)
                dve.wait_ge(chain_dve, linked[0])

            def split(val, part, done):
                link(V.tensor_tensor(val, val, part(0), ALU.subtract))
                V.tensor_copy(part(1), val).then_inc(done, 1)
                dve.wait_ge(done, 2)
                V.tensor_tensor(part(2), val, part(1), ALU.subtract).then_inc(done, 1)

            def variance(tiles):
                for i in tiles:
                    ins = V.bn_stats(stats[:, i, :], z[:, i, :])
                link(ins)
                for i in tiles:
                    ins = V.bn_aggr(mv[:, i, :], stats[:, i, :])
                ins.then_inc(s_var, 1)

            def norm(tiles, n, dst):
                dve.wait_ge(s_rstd, n + 1)
                for i in tiles:
                    ins = V.tensor_scalar(dst[:, i, :], z[:, i, :], mv[:, i, 0:1], rstd[:, n, i:i + 1],
                                          ALU.subtract, ALU.mult)
                return ins

            V.memset(warm[:], 0.0).then_inc(s_warm, 1)
            V.memset(words(q_stack["A"][:, :, 0:T]), 0.0).then_inc(cleared["qA0"], 1)
            V.memset(words(k_stack_a[MROW:MROW + 32, :]), ONES).then_inc(cleared["kA"], 1)
            dve.wait_ge(ld_first, 16)
            V.tensor_scalar(bias_col[:, 0:3], bias_col[:, 0:3], SCALE, None, ALU.mult).then_inc(s_bias, 1)
            for b in range(B):
                cols = slice(b * T, (b + 1) * T)
                wait_emptied(dve, ("qA", b))
                split(val_q[:, cols], lambda r: part_q[:, r, cols], s_parts[f"qA{b}"])
                wait_emptied(dve, ("kA", b))
                link(V.tensor_tensor(val_k[:, cols], val_k[:, cols], part_k[:, 0, cols], ALU.subtract))
                V.tensor_copy(k_stack_a[32:64, cols], val_k[32:64, cols]).then_inc(s_stack[f"kA{b}"], 1)
                link(V.tensor_copy(part_k[:, 1, cols], val_k[:, cols]))
                V.tensor_tensor(k_stack_a[96:128, cols], val_k[96:128, cols], part_k[96:128, 1, cols],
                                ALU.subtract).then_inc(s_stack[f"kA{b}"], 1)
            dve.wait_ge(ld_row, 16)
            dve.wait_ge(cleared["vA"], 1)
            o = wait_full(dve, "vA")
            ins = V.tensor_tensor(v_a[:, :, 0:D], o[:, 0:4 * D].rearrange("p (i d) -> p i d", d=D),
                                  bias_row[:, 0:1, 0:D].to_broadcast([P, 4, D]), ALU.add)
            emptied(ins, "vA")

            n_norm = 0
            for s in steps:
                kind = s[0]
                if kind == "S":
                    _, part, b, g, h, qt = s
                    mb = mb_of[(part, b, g)]
                    o = wait_full(dve, s)
                    if part == "A":
                        dst, src = mneg[:, mb, 0:2, h], o[:].rearrange("p (a k) -> p a k", a=2)
                    elif part == "B":
                        dst, src = mneg[:, mb, :, h], o[:, 0:3 * P].rearrange("p (a k) -> p a k", a=3)
                    else:
                        dst, src = mneg[:, mb, qt, h:h + 1], o[:]
                    emptied(V.tensor_reduce(out=dst, in_=src, axis=AX.X, op=ALU.max, negate=True), s)
                    last_s = s
                elif kind == "MS":
                    mb = mb_of[s[1:4]]
                    wait_emptied(dve, last_s)
                    if s[1] == "B":
                        link(V.tensor_tensor(mneg[:, mb, 1, :], mneg[:, mb, 1, :], mneg[:, mb, 2, :], ALU.min))
                    link(V.tensor_copy(mpart[:, mb, :, 0, :], mneg[:, mb, 0:2, :]))
                    link(V.tensor_tensor(mneg[:, mb, 0:2, :], mneg[:, mb, 0:2, :], mpart[:, mb, :, 0, :], ALU.subtract))
                    link(V.tensor_copy(mpart[:, mb, :, 1, :], mneg[:, mb, 0:2, :]))
                    V.tensor_tensor(mpart[:, mb, :, 2, :], mneg[:, mb, 0:2, :], mpart[:, mb, :, 1, :],
                                    ALU.subtract).then_inc(s_mpart, 1)
                    if s[1:] == ("A", 1, 1):
                        dve.wait_ge(ld_b1, 16)
                        V.tensor_copy(b1_part[0], b1_sb).then_inc(s_parts["b1"], 1)
                        dve.wait_ge(s_parts["b1"], 1)
                        split(b1_sb, lambda r: b1_part[r], s_parts["b1"])
                elif kind == "MT":
                    mb = mb_of[s[1:4]]
                    if mb >= NROW:
                        dve.wait_ge(s_shift[mb - NROW], 16)
                    o = wait_full(dve, s).bitcast(BF16)
                    emptied(V.tensor_copy(mrow[:, mb % NROW, :], o[0:24, 0:T]), s)
                elif kind == "VC":
                    dve.wait_ge(cleared["vC"], 1)
                    o = wait_full(dve, s)
                    for i in range(4):
                        ins = V.tensor_tensor(head_values(v_c[:, 4 * s[1] + i, :]),
                                              o[:, i * P:(i + 1) * P].rearrange("p (h d) -> p h d", d=D),
                                              bias_row[:, 2, :].rearrange("p (h d) -> p h d", d=D), ALU.add)
                    emptied(ins, s)
                elif kind == "TY":
                    _, part, b = s
                    o = wait_full(dve, s).rearrange("p (n w) -> p n w", w=VW)
                    link(V.reciprocal(ysum[:], o[:, :, D:D + 1]))
                    dst = ytok[:, b if part == CROSS_ORDER[b][0] or part == "A" else B, :].rearrange("p (n d) -> p n d", d=D)
                    emptied(V.tensor_tensor(dst, o[:, :, 0:D], ysum[:].to_broadcast([P, 32, D]), ALU.mult), s)
                    wait_emptied(dve, s)
                    if part == CROSS_ORDER[b][1]:
                        V.tensor_tensor(ytok[:, b, :], ytok[:, b, :], ytok[:, B, :], ALU.add).then_inc(s_ytok, 1)
                elif kind == "YT":
                    o = wait_full(dve, s)
                    emptied(V.tensor_copy(yT[:], o[:, 0:T]), s)
                elif kind == "WO":
                    _, b, cross = s
                    dve.wait_ge(s_xres, 1 if not cross else 2 + b)
                    o = wait_full(dve, s)
                    ins = V.tensor_tensor(z[:], o[:, 0:T].rearrange("p (i c) -> p i c", c=C),
                                          xpb[:, 2 * b:2 * b + 2, :], ALU.add)
                    emptied(ins, s)
                    wait_emptied(dve, s)
                    variance(range(QT))
                elif kind == "LN":
                    _, b, cross = s
                    dve.wait_ge(s_parts["b1"], 3)
                    norm(range(QT), n_norm, (x2 if cross else x1)[:, 2 * b:2 * b + 2, :]).then_inc(s_xn, 1)
                    n_norm += 1
                elif kind == "XT":
                    _, b, cross = s
                    o = wait_full(dve, s)
                    emptied(V.tensor_copy((x2T if cross else x1T)[:, b * T:(b + 1) * T], o[:, 0:T]), s)
                elif kind == "PROJ":
                    b = s[1]
                    cols = slice(b * T, (b + 1) * T)
                    wait_emptied(dve, ("q", b))
                    split(val_q[:, cols], lambda r: part_q[:, r, cols], s_parts[f"qB{b}"])
                    o = wait_full(dve, ("qcv", b))
                    link(V.tensor_scalar(val_qc[:, cols], o[:, 0:T], SCALE, bias_col[:, 2:3], ALU.mult, ALU.add))
                    dve.wait_ge(cleared["vB"], 1)
                    for i in range(QT):
                        ins = V.tensor_tensor(head_values(v_b[:, 2 * b + i, :]),
                                              o[:, T + i * C:T + (i + 1) * C].rearrange("p (h d) -> p h d", d=D),
                                              bias_row[:, 1, :].rearrange("p (h d) -> p h d", d=D), ALU.add)
                    emptied(ins, ("qcv", b))
                    V.tensor_copy(part_qc[:, 0, cols], val_qc[:, cols]).then_inc(s_parts[f"qC{b}"], 1)
                    dve.wait_ge(s_parts[f"qC{b}"], 1)
                    split(val_qc[:, cols], lambda r: part_qc[:, r, cols], s_parts[f"qC{b}"])
                elif kind == "GATE":
                    b = s[1]
                    t = {k: gate[:, b, n, :, :] for n, k in enumerate(
                        ("logit", "stat", "small", "exp", "score", "top", "index", "weight", "one0", "one1", "comb"))}
                    small = lambda n: t["small"][:, :, n:n + 1]
                    o = wait_full(dve, s)
                    V.tensor_reduce(out=t["stat"][:, :, 0], in_=o[:, 0:QT * E].rearrange("p (i e) -> p i e", e=E),
                                    axis=AX.X, op=ALU.max, negate=True).then_inc(s_lmax, 1)
                    wait_emptied(dve, s)
                    link(V.reciprocal(small(0), t["stat"][:, :, 1:2]))
                    link(V.tensor_tensor(t["score"], t["exp"], small(0).to_broadcast([P, QT, E]), ALU.mult))
                    for i in range(QT):
                        ins = V.max(out=t["top"][:, i, :], in_=t["score"][:, i, :])
                    link(ins)
                    for i in range(QT):
                        ins = V.max_index(gate_i[:, b, i, :], t["top"][:, i, :], t["score"][:, i, :])
                    link(ins)
                    link(V.tensor_copy(t["index"], gate_i[:, b]))
                    link(V.tensor_tensor(small(1), t["top"][:, :, 0:1], t["top"][:, :, 1:2], ALU.add))
                    link(V.tensor_scalar(small(2), small(1), EPS_TOP, None, ALU.add))
                    link(V.reciprocal(small(3), small(2)))
                    link(V.tensor_tensor(t["weight"][:, :, 0:2], t["top"][:, :, 0:2],
                                         small(3).to_broadcast([P, QT, 2]), ALU.mult))
                    link(V.tensor_tensor(small(4), t["weight"][:, :, 0:1], t["weight"][:, :, 1:2], ALU.add))
                    link(V.tensor_scalar(t["weight"][:, :, 2:4], t["weight"][:, :, 0:2], 0.5, None, ALU.mult))
                    for i in range(QT):
                        for k in range(2):
                            ins = V.tensor_scalar(t[f"one{k}"][:, i, :], expert_no[:], t["index"][:, i, k:k + 1],
                                                  t["weight"][:, i, 2 + k:3 + k], ALU.is_equal, ALU.mult)
                    link(ins)
                    link(V.tensor_tensor(t["comb"], t["one0"], t["one1"], ALU.add))
                elif kind == "F":
                    _, b, e, t = s
                    n = f_of[s[1:]]
                    dve.wait_ge(s_tanh, n + 1)
                    o = wait_full(dve, s)
                    product = gated[:, n % 2, :]
                    emptied(V.scalar_tensor_tensor(out=product, in0=tanh_b[:, n % 4, :], scalar=1.0, in1=o[:, 0:HF],
                                                   op0=ALU.add, op1=ALU.mult), s)
                    if (e, t) == (1, 0):
                        for i in range(QT):
                            ins = V.scalar_tensor_tensor(out=xpb[:, 2 * b + i, :], in0=bias_row[:, 5, :],
                                                         scalar=gate[:, b, 2, i, 4:5], in1=x2[:, 2 * b + i, :],
                                                         op0=ALU.mult, op1=ALU.add)
                        link(ins)
                    wait_emptied(dve, s)
                    dst = gsum[:, b, t, :]
                    weight = gate[:, b, 10, t, e:e + 1]
                    if e == 0:
                        ins = V.tensor_scalar(dst, product, weight, None, ALU.mult)
                    else:
                        dve.wait_ge(s_gated, n)
                        ins = V.scalar_tensor_tensor(out=dst, in0=product, scalar=weight, in1=dst,
                                                     op0=ALU.mult, op1=ALU.add)
                    ins.then_inc(s_gated, 1)
                elif kind == "GT":
                    o = wait_full(dve, s)
                    emptied(V.tensor_copy(gT[s[1]][:, s[2], :], o[:, 0:HF]), s)
                elif kind == "OUT":
                    _, b, t = s
                    o = wait_full(dve, s)
                    emptied(V.tensor_tensor(z[:, t, :], o[:, 0:C], xpb[:, 2 * b + t, :], ALU.add), s)
                    wait_emptied(dve, s)
                    variance(range(t, t + 1))
                    norm(range(t, t + 1), n_norm, fin[:, 2 * b:2 * b + 2, :]).then_inc(s_fin, 1)
                    n_norm += 1

        @block.scalar
        def _(act):
            A = nc.scalar
            act.wait_ge(s_warm, 1)
            A.activation(warm[:], warm[:], ACT.Exp)
            act.wait_ge(s_bias, 1)
            for b in range(B):
                cols = slice(b * T, (b + 1) * T)
                o = wait_full(act, ("qA", b))
                A.activation(part_q[:, 0, cols], o[:, 0:T], ACT.Identity, bias=bias_col[:, 0:1],
                             scale=SCALE).then_inc(s_parts[f"qA{b}"], 1)
                emptied(A.activation(val_q[:, cols], o[:, 0:T], ACT.Identity, bias=bias_col[:, 0:1], scale=SCALE),
                        ("qA", b))
                o = wait_full(act, ("kA", b))
                A.activation(k_stack_a[0:32, cols], o[0:32, 0:T], ACT.Copy).then_inc(s_stack[f"kA{b}"], 1)
                A.activation(part_k[:, 0, cols], o[:, 0:T], ACT.Copy)
                emptied(A.activation(val_k[:, cols], o[:, 0:T], ACT.Copy), ("kA", b))
            o = wait_full(act, "kC")
            A.activation(part_c[:, 0, :], o[:], ACT.Identity, bias=bias_col[:, 4:5]).then_inc(s_parts["kC"], 1)
            emptied(A.activation(val_c, o[:], ACT.Identity, bias=bias_col[:, 4:5]), "kC")

            for s in steps:
                kind = s[0]
                if kind == "U":
                    n = unit_of[s[1:]]
                    if n >= NPT:
                        act.wait_ge(s_pv, unit_pv[n - NPT] + 1)
                    o = wait_full(act, s)
                    dst = probs[:, n % NPT, :]
                    if s[1] == "B":
                        ins = A.activation(dst.rearrange("p (i c) -> p i c", i=2)[:, :, 0:T + P],
                                           o[:].rearrange("p (i c) -> p i c", i=2)[:, :, 0:T + P], ACT.Exp)
                    else:
                        ins = A.activation(dst, o[:], ACT.Exp)
                    emptied(ins, s)
                elif kind == "PV" and s[4:] == (0 if s[1] == "A" else 1, last_kt[s[1]]):
                    part, b, g, hh = s[1:5]
                    if (part, b, g) == ("A", 1, 0):
                        act.wait_ge(s_stack["kC"], STACKED)
                    if (part, b, g) == ("C", 0, 1):
                        act.wait_ge(s_stack["b1"], 48)
                    act.wait_ge(s_pv, pv_of[s[1:5]] + 1)
                    emptied(A.activation(y_slot(part, b, g), region["y"][:], ACT.Copy), ("Y", part, b, g))
                elif kind == "PROJ":
                    b = s[1]
                    cols = slice(b * T, (b + 1) * T)
                    o = wait_full(act, ("q", b))
                    act.wait_ge(s_stack[f"qA{b}"], STACKED)
                    A.activation(part_q[:, 0, cols], o[:, 0:T], ACT.Identity, bias=bias_col[:, 1:2],
                                 scale=SCALE).then_inc(s_parts[f"qB{b}"], 1)
                    emptied(A.activation(val_q[:, cols], o[:, 0:T], ACT.Identity, bias=bias_col[:, 1:2], scale=SCALE),
                            ("q", b))
                    o = wait_full(act, ("k", b))
                    act.wait_ge(s_stack[f"kA{b}"], 3)
                    A.activation(part_k[:, 0, cols], o[:, 0:T], ACT.Identity,
                                 bias=bias_col[:, 3:4]).then_inc(s_parts[f"kB{b}"], 1)
                    emptied(A.activation(val_k[:, cols], o[:, 0:T], ACT.Identity, bias=bias_col[:, 3:4]), ("k", b))
                elif kind == "GATE":
                    b = s[1]
                    act.wait_ge(s_lmax, b + 1)
                    o = wait_full(act, s)
                    for i in range(QT):
                        ins = A.activation(gate[:, b, 3, i, :], o[:, i * E:(i + 1) * E], ACT.Exp,
                                           bias=gate[:, b, 1, i, 0:1], accum_out=gate[:, b, 1, i, 1:2])
                    emptied(ins, s)
                elif kind == "F":
                    n = f_of[s[1:]]
                    if n >= 4:
                        wait_emptied(act, f_steps[n - 4])
                    o = wait_full(act, s)
                    A.activation(tanh_b[:, n % 4, :], o[:, HF:2 * HF], ACT.Tanh, scale=0.5).then_inc(s_tanh, 1)

        @block.gpsimd
        def _(pool):
            G = nc.gpsimd
            linked = [0]

            def link(ins):
                linked[0] += 1
                ins.then_inc(chain_pool, 1)
                pool.wait_ge(chain_pool, linked[0])

            def split(val, part, done):
                link(G.tensor_tensor(val, val, part(0), ALU.subtract))
                G.tensor_copy(part(1), val).then_inc(done, 1)
                pool.wait_ge(done, 2)
                G.tensor_tensor(part(2), val, part(1), ALU.subtract).then_inc(done, 1)

            link(G.memset(ident[:], 0.0))
            G.affine_select(out=ident[:], in_=ident[:], compare_op=ALU.not_equal, fill=1.0, base=0,
                            pattern=[[-1, P]], channel_multiplier=1).then_inc(s_ident, 1)
            G.memset(words(q_stack["A"][:, :, T:N]), 0.0).then_inc(cleared["qA1"], 1)
            link(G.memset(ident_bf[:], 0.0))
            G.affine_select(out=ident_bf[:], in_=ident_bf[:], compare_op=ALU.not_equal, fill=1.0, base=0,
                            pattern=[[-1, P]], channel_multiplier=1).then_inc(s_ident_bf, 1)
            G.memset(mask_q[:], 0.0)
            link(G.memset(mask_k[:], 0.0))
            G.affine_select(out=mask_q[:], in_=mask_q[:], compare_op=ALU.is_ge, fill=NEG, base=0,
                            pattern=[[-1, P]], channel_multiplier=1)
            G.affine_select(out=mask_k[:], in_=mask_k[:], compare_op=ALU.is_ge, fill=NEG, base=0,
                            pattern=[[1, P]], channel_multiplier=-1).then_inc(s_mask, 1)
            G.memset(v_a[:], 1.0).then_inc(cleared["vA"], 1)
            G.memset(words(k_stack_c[:]), ONES).then_inc(cleared["kC"], 1)
            G.memset(v_c[:], 1.0).then_inc(cleared["vC"], 1)
            wait_emptied(pool, "kC")
            split(val_c, lambda r: part_c[:, r, :], s_parts["kC"])
            pool.wait_ge(cleared["kC"], 1)
            make_stack(pool, lambda r: k_stack_c[r, :, :], part_c, 1, "kC")
            pool.wait_ge(ld_row, 16)
            pool.wait_ge(ld_rest, 16)
            for i in range(N // P):
                ins = G.tensor_tensor(xpb[:, i, :], x_sb[:, i, :], bias_row[:, 3, :], ALU.add)
            ins.then_inc(s_xres, 1)
            G.memset(half_neg[:], -0.5)
            for e in range(E):
                ins = G.memset(expert_no[:, e:e + 1], float(e))
            ins.then_inc(s_small, 1)
            G.memset(words(q_stack["B"][:]), 0.0).then_inc(cleared["qB"], 1)
            G.memset(words(k_stack_b[:]), ONES).then_inc(cleared["kB"], 1)
            G.memset(v_b[:], 1.0).then_inc(cleared["vB"], 1)
            link(G.memset(bias_sel[:], 0.0))
            for r in range(3):
                ins = G.affine_select(out=bias_sel[:], in_=bias_sel[:], compare_op=ALU.not_equal, fill=1.0,
                                      base=-8 * r, pattern=[[-1, E], [0, P]], channel_multiplier=1)
                if r < 2:
                    link(ins)
            ins.then_inc(s_sel, 1)
            n_norm = 0
            for s in steps:
                kind = s[0]
                if kind in ("WO", "OUT"):
                    pool.wait_ge(s_var, n_norm + 1)
                    i = slice(s[2], s[2] + 1) if kind == "OUT" else slice(0, QT)
                    link(G.tensor_scalar(rstd[:, n_norm, i], mv[:, i, 1], EPS_LN, None, ALU.add))
                    G.tensor_tensor(rstd[:, n_norm, i], rstd[:, n_norm, i], half_neg[:, i], ALU.pow).then_inc(s_rstd, 1)
                    n_norm += 1
                elif kind == "XT" and not s[2]:
                    b = s[1]
                    pool.wait_ge(s_xn, xt_of[(b, 0)] + 1)
                    for i in range(QT):
                        ins = G.tensor_tensor(xpb[:, 2 * b + i, :], x1[:, 2 * b + i, :], bias_row[:, 4, :], ALU.add)
                    ins.then_inc(s_xres, 1)
                elif kind == "PROJ":
                    b = s[1]
                    cols = slice(b * T, (b + 1) * T)
                    wait_emptied(pool, ("k", b))
                    split(val_k[:, cols], lambda r: part_k[:, r, cols], s_parts[f"kB{b}"])
                    pool.wait_ge(cleared["kB"], 1)
                    make_stack(pool, lambda r: k_stack_b[r, :, cols], part_k[:, :, cols], 1, f"kB{b}", (1, 2),
                               s_stack_low[b])
                    pool.wait_ge(s_pv, pv_of[("A", b, 1, 0)] + 1)
                    pool.wait_ge(s_parts[f"kB{b}"], 3)
                    G.memset(words(q_stack["C"][2 * 32:3 * 32, :, cols]), 0.0).then_inc(cleared[f"qC{b}"], 1)
                    pool.wait_ge(cleared[f"qC{b}"], 1)
                    if b == 1:
                        make_stack(pool, lambda r: q_stack["C"][r, :, cols], part_qc[:, :, cols], 0, f"qC{b}")

        @block.sync
        def _(sp):
            sp.dma_start(first[0][:], packs["first_0"]).then_inc(ld_first, 16)
            sp.dma_start(first[1][:], packs["first_1"]).then_inc(ld_second, 16)
            sp.dma_start(ctx_pack, packs["ctx"]).then_inc(ld_ctx, 16)
            sp.dma_start(bias_row[:].rearrange("p n c -> p (n c)"), packs["rows"].partition_broadcast(P)).then_inc(ld_row, 16)

            stored = 0
            for b in range(B):
                cols = slice(b * T, (b + 1) * T)
                sp.wait_ge(cleared[f"qA{b}"], 1)
                make_stack(sp, lambda r: q_stack["A"][r, :, cols], part_q[:, :, cols], 0, f"qA{b}")
            sp.dma_start(b1_sb, packs["b1"]).then_inc(ld_b1, 16)
            sp.dma_start(rest[:], packs["rest"]).then_inc(ld_rest, 16)
            sp.dma_start(w1T[:].rearrange("p e n -> p (e n)"), packs["w1T"]).then_inc(ld_w1, 16)

            for s in steps:
                kind = s[0]
                if kind == "MT":
                    _, part, b, g = s
                    mb = mb_of[s[1:4]]
                    wait_emptied(sp, s)
                    sp.dma_start(q_stack[part][MROW:MROW + 3, 8 * g:8 * g + 8, b * T:(b + 1) * T],
                                 mrow[:, mb % NROW, :]).then_inc(s_shift[mb], 16)
                elif kind == "PROJ":
                    b = s[1]
                    cols = slice(b * T, (b + 1) * T)
                    sp.wait_ge(cleared["qB"], 1)
                    make_stack(sp, lambda r: q_stack["B"][r, :, cols], part_q[:, :, cols], 0, f"qB{b}")
                    sp.wait_ge(cleared["kB"], 1)
                    make_stack(sp, lambda r: k_stack_b[r, :, cols], part_k[:, :, cols], 1, f"kB{b}", (0,))
                    if b == 0:
                        sp.wait_ge(cleared[f"qC{b}"], 1)
                        make_stack(sp, lambda r: q_stack["C"][r, :, cols], part_qc[:, :, cols], 0, f"qC{b}")
                        sp.wait_ge(s_parts["b1"], 3)
                        for r in range(3):
                            sp.dma_start(b1_stack[E * r:E * r + E, :], b1_part[r]).then_inc(s_stack["b1"], 16)
                elif kind == "OUT":
                    _, b, t = s
                    stored += 1
                    sp.wait_ge(s_fin, stored)
                    sp.dma_start(out[b, t * P:(t + 1) * P, :], fin[:, 2 * b + t, :]).then_inc(s_store, 16)
            sp.wait_ge(s_store, 16 * stored)


def kernel(**inputs):
    import numpy as _np
    import concourse.bacc as _bacc
    from concourse import mybir as _mybir
    from concourse.bass_utils import run_bass_kernel_spmd as _run

    i = {k: _np.asarray(v) for k, v in inputs.items()}
    order = _np.arange(C).reshape(H, D).T.ravel()
    col = lambda k, o=slice(None): i[k][o].reshape(C, 1)
    xT = i["x"].transpose(2, 0, 1)
    bv = _np.zeros(C, i["L0_attn_bv"].dtype)
    bv[:D] = i["L0_attn_bv"]
    packs = {
        "first_0": [xT[:, 0], i["L0_attn_Wq"].T[:, order], _np.tile(i["L0_attn_Wk"].T, H), i["L0_attn_Wv"].T,
                    col("L0_attn_bq", order), col("L0_xattn_bq", order), col("L0_xattn_bcq", order),
                    col("L0_xattn_bk", order), col("L0_xattn_bck", order)],
        "first_1": [xT[:, 1]],
        "ctx": [i["ctx_512"].transpose(2, 0, 1).reshape(CC, B * TC), i["L0_xattn_Wck"][:, order], i["L0_xattn_Wcv"]],
        "rest": [i["x"].reshape(N // P, P, C).transpose(1, 0, 2).reshape(P, N),
                 i["L0_xattn_Wq"][:, order], i["L0_xattn_Wk"][:, order], i["L0_xattn_Wcq"][:, order],
                 i["L0_xattn_Wv"], i["L0_xattn_Wp"], i["L0_attn_Wo"].T,
                 i["L0_ffn_Wo"].T[:P], i["L0_ffn_Wo"].T[P:], i["L0_ffn_Wg"].T],
        "w1T": [i["L0_ffn_W1"].transpose(2, 0, 1).reshape(P, E * 2 * HF)],
        "b1": [i["L0_ffn_b1"]],
        "rows": [bv, i["L0_xattn_bv"], i["L0_xattn_bcv"], i["L0_attn_bo"], i["L0_xattn_bp"], i["L0_ffn_bo"]],
    }
    packs = {k: _np.ascontiguousarray(_np.concatenate(v, axis=-1)) for k, v in packs.items()}

    nc = _bacc.Bacc("TRN2", target_bir_lowering=False, num_devices=1)
    aps = {k: nc.dram_tensor(f"in_{k}", a.shape, _mybir.dt.from_np(a.dtype), kind="ExternalInput").ap()
           for k, a in packs.items()}
    out = nc.dram_tensor("out_0", (B, T, C), _mybir.dt.float32, kind="ExternalOutput").ap()
    build(nc, aps, out)
    r = _run(nc, [{f"in_{k}": a for k, a in packs.items()}], core_ids=[0])
    return r.results[0]["out_0"]
```
